# Optimizing a Trainium2 kernel written in Bass

```python
import numpy as np
import jax
import jax.numpy as jnp

def _softmax(x, axis=-1):
    return jax.nn.softmax(x, axis=axis)

def _gelu(x):
    return jax.nn.gelu(x, approximate=True)

def _silu(x):
    return jax.nn.silu(x)

def _sigmoid(x):
    return jax.nn.sigmoid(x)

def _layernorm(x, axis=-1, eps=1e-05):
    m = jnp.mean(x, axis=axis, keepdims=True)
    v = jnp.var(x, axis=axis, keepdims=True)
    return (x - m) / jnp.sqrt(v + eps)

def _scatter_add(tgt, idx, src, axis=0):
    return tgt.at[idx].add(src)

def _segment_sum(src, seg, n):
    return jax.ops.segment_sum(src, seg, n)
kernel_name = 'mk_adj_resnorm_d4_adj_r2_9a5f46'

def setup_inputs(seed: int=0):
    np.random.seed(seed)
    _w = jnp.asarray

    def _rec_inputs():
        import jax
        import jax.numpy as jnp
        _gk = jax.random.key(seed)
        x = -0.0003929 + 0.9999 * jax.random.normal(jax.random.fold_in(_gk, 1), (32, 256, 256), jnp.float32)
        _a = jax.random.bernoulli(jax.random.fold_in(_gk, 2), 0.015625, (32, 256, 256))
        _a = jnp.logical_or(_a, jnp.eye(256, dtype=bool))
        _af = _a.astype(jnp.float32)
        _af = _af * jax.random.uniform(jax.random.fold_in(_gk, 3), (32, 256, 256), jnp.float32, 0.05, 1)
        adj = _af
        return (x, adj)
    x, adj = _rec_inputs()

    def _L0_gnn_setup():
        import jax, jax.numpy as jnp
        import numpy as np
        B, N, C_IN, C_OUT = (8, 2048, 256, 256)
        key = jax.random.key(seed)
        k1, k2, k3, k4 = jax.random.split(key, 4)
        node_features = jax.random.normal(k1, (B, N, C_IN), dtype=jnp.float32)
        adj_matrix = jax.random.uniform(k2, (B, N, N), dtype=jnp.float32)
        W = jax.random.normal(k3, (C_IN, C_OUT), dtype=jnp.float32) / np.sqrt(C_IN)
        b = jax.random.normal(k4, (C_OUT,), dtype=jnp.float32) * 0.01
        return {'node_features': node_features, 'adj_matrix': adj_matrix, 'W': W, 'b': b}
    _L0_gnn_all = _L0_gnn_setup()
    _L0_gnn_in = {k: v for k, v in _L0_gnn_all.items() if k in ('W', 'b')}
    del _L0_gnn_all

    def _L1_gnn_setup():
        import jax, jax.numpy as jnp
        import numpy as np
        key = jax.random.key(seed)
        k1, k2, k3 = jax.random.split(key, 3)
        B, N, F, D = (8, 1024, 256, 256)
        x = jax.random.normal(k1, (B, N, F), dtype=jnp.float32)
        a = jax.random.uniform(k2, (B, N, N), dtype=jnp.float32)
        kernel = jax.random.normal(k3, (F, D), dtype=jnp.float32) * (1.0 / np.sqrt(F))
        return {'x': x, 'a': a, 'kernel': kernel}
    _L1_gnn_all = _L1_gnn_setup()
    _L1_gnn_in = {k: v for k, v in _L1_gnn_all.items() if k in ('kernel',)}
    del _L1_gnn_all

    def _L2_gnn_setup():
        import jax, jax.numpy as jnp
        import numpy as np
        N = 4096
        F = 256
        C = 256
        key = jax.random.key(seed)
        k1, k2, k3 = jax.random.split(key, 3)
        X = jax.random.normal(k1, (1, N, F), dtype=jnp.float32)
        A = jax.random.uniform(k2, (1, N, N), dtype=jnp.float32)
        kernel = jax.random.normal(k3, (F, C), dtype=jnp.float32) * (1.0 / np.sqrt(F))
        bias = jnp.zeros((C,), dtype=jnp.float32)
        return {'X': X, 'A': A, 'kernel': kernel, 'bias': bias}
    _L2_gnn_all = _L2_gnn_setup()
    _L2_gnn_in = {k: v for k, v in _L2_gnn_all.items() if k in ('kernel', 'bias')}
    del _L2_gnn_all

    def _L3_gnn_setup():
        import jax, jax.numpy as jnp
        import numpy as np
        B, N, DIN, DOUT, K = (4, 1024, 256, 256, 3)
        key = jax.random.key(seed)
        ks = jax.random.split(key, 8)
        X = jax.random.normal(ks[0], (B, N, DIN), dtype=jnp.float32)
        A = jax.random.uniform(ks[1], (B, N, N), dtype=jnp.float32)
        Wv = jax.random.normal(ks[2], (DIN, DOUT), dtype=jnp.float32) * 0.02
        bv = jax.random.normal(ks[3], (DOUT,), dtype=jnp.float32) * 0.02
        aw = jax.random.normal(ks[4], (2 * DOUT, 1), dtype=jnp.float32) * 0.05
        ab = jax.random.normal(ks[5], (1,), dtype=jnp.float32) * 0.05
        Wk = jax.random.normal(ks[6], (K, DIN, DOUT), dtype=jnp.float32) * 0.02
        bk = jax.random.normal(ks[7], (K, DOUT), dtype=jnp.float32) * 0.02
        return {'X': X, 'A': A, 'Wv': Wv, 'bv': bv, 'aw': aw, 'ab': ab, 'Wk': Wk, 'bk': bk}
    _L3_gnn_all = _L3_gnn_setup()
    _L3_gnn_in = {k: v for k, v in _L3_gnn_all.items() if k in ('Wv', 'bv', 'aw', 'ab', 'Wk', 'bk')}
    del _L3_gnn_all
    return {'x': x, 'adj': adj, 'L0_gnn_W': _L0_gnn_in['W'], 'L0_gnn_b': _L0_gnn_in['b'], 'L1_gnn_kernel': _L1_gnn_in['kernel'], 'L2_gnn_kernel': _L2_gnn_in['kernel'], 'L2_gnn_bias': _L2_gnn_in['bias'], 'L3_gnn_Wv': _L3_gnn_in['Wv'], 'L3_gnn_bv': _L3_gnn_in['bv'], 'L3_gnn_aw': _L3_gnn_in['aw'], 'L3_gnn_ab': _L3_gnn_in['ab'], 'L3_gnn_Wk': _L3_gnn_in['Wk'], 'L3_gnn_bk': _L3_gnn_in['bk']}

def reference(x, adj, L0_gnn_W, L0_gnn_b, L1_gnn_kernel, L2_gnn_kernel, L2_gnn_bias, L3_gnn_Wv, L3_gnn_bv, L3_gnn_aw, L3_gnn_ab, L3_gnn_Wk, L3_gnn_bk):
    import jax
    import jax.numpy as jnp

    def _L0_gnn_ref(node_features, adj_matrix, W, b):
        import jax, jax.numpy as jnp
        import numpy as np
        B, N, C_IN, C_OUT = (8, 2048, 256, 256)
        num_neighbours = adj_matrix.sum(axis=-1, keepdims=True)
        h = jnp.einsum('bni,io->bno', node_features, W) + b
        h = jnp.einsum('bnm,bmo->bno', adj_matrix, h)
        return h / num_neighbours

    def _L1_gnn_ref(x, a, kernel):
        import jax, jax.numpy as jnp
        import numpy as np
        t = jnp.einsum('bnm,bmf->bnf', a, x)
        out = jnp.einsum('bnf,fd->bnd', t, kernel)
        out = jax.nn.relu(out)
        mask = (jnp.sum((x != 0).astype(jnp.float32), axis=-1, keepdims=True) > 0).astype(jnp.float32)
        return out * mask

    def _L2_gnn_ref(X, A, kernel, bias):
        import jax, jax.numpy as jnp
        import numpy as np
        N = 4096
        F = 256
        C = 256
        Ah = A + jnp.eye(A.shape[-1], dtype=A.dtype)[None, :, :]
        dh = jax.lax.rsqrt(jnp.sum(Ah, axis=-1))
        An = dh[:, :, None] * Ah * dh[:, None, :]
        out = jnp.einsum('bnm,bmf,fc->bnc', An, X, kernel) + bias
        return jax.nn.relu(out)

    def _L3_gnn_ref(X, A, Wv, bv, aw, ab, Wk, bk):
        import jax, jax.numpy as jnp
        import numpy as np
        B, N, DIN, DOUT, K = (4, 1024, 256, 256, 3)
        d = Wv.shape[1]
        Xw = X @ Wv + bv
        sj = Xw @ aw[:d, 0]
        si = Xw @ aw[d:, 0]
        e = jax.nn.leaky_relu(sj[:, None, :] + si[:, :, None] + ab[0], negative_slope=0.2)
        alpha_matrix = A * jnp.exp(e)
        transition = alpha_matrix / (jnp.sum(alpha_matrix, axis=-1, keepdims=True) + 1e-12)
        H = jnp.zeros(X.shape[:-1] + (d,), dtype=X.dtype)
        Xk = X
        for k in range(Wk.shape[0]):
            H = H + Xk @ Wk[k] + bk[k]
            Xk = jnp.einsum('bij,bjd->bid', transition, Xk)
        return jax.nn.relu(H)
    x = _layernorm(x + _L0_gnn_ref(x, adj, L0_gnn_W, L0_gnn_b), axis=-1)
    x = _layernorm(x + _L1_gnn_ref(x, adj, L1_gnn_kernel), axis=-1)
    x = _layernorm(x + _L2_gnn_ref(x, adj, L2_gnn_kernel, L2_gnn_bias), axis=-1)
    x = _layernorm(x + _L3_gnn_ref(x, adj, L3_gnn_Wv, L3_gnn_bv, L3_gnn_aw, L3_gnn_ab, L3_gnn_Wk, L3_gnn_bk), axis=-1)
    return x

_drawn_inputs = setup_inputs


def setup_inputs(seed=0):
    import zlib

    import numpy as np

    out = dict(_drawn_inputs(seed))
    spreads = {'L2_gnn_bias': (0.0, 0.1)}
    factors = {'L0_gnn_b': 4.16, 'L3_gnn_Wv': 2.929, 'L3_gnn_bv': 8.0, 'L3_gnn_aw': 3.241}
    for name, (base, spread) in spreads.items():
        noise = np.random.default_rng([zlib.crc32(name.encode()), seed]).standard_normal(out[name].shape)
        drawn = base * np.exp(spread * noise) if base else spread * noise
        out[name] = jnp.asarray(drawn.astype(out[name].dtype))
    for name, factor in factors.items():
        out[name] = (out[name] * factor).astype(out[name].dtype)
    return out
```

```python
from contextlib import ExitStack

import concourse.bass as bass
from concourse import mybir

P = 128
SLOTS = 4
EPS = 1e-5
FP = mybir.dt.float32
FR = mybir.dt.float32r
ALU = mybir.AluOpType
ACT = mybir.ActivationFunctionType


def build(nc, x, xT, adjT, w0, w1, w2, wk, wvT, aw, bv, ab, b0, b2, bk, out):
    B = x.shape[0]
    N = x.shape[2] // 2
    F = N
    GROUPS = B // SLOTS
    C = 2 * N
    FA = F + 2

    with ExitStack() as ctx:
        def sb(name, shape, dt=FP):
            return ctx.enter_context(nc.sbuf_tensor(name, shape, dt))

        def sem(name):
            return ctx.enter_context(nc.semaphore(name))

        def sem4(name):
            return [sem(f"{name}{g}") for g in range(SLOTS)]

        def slots(name, cols, dt=FP):
            return [sb(f"{name}{g}", [P, cols], dt) for g in range(SLOTS)]

        W0 = [sb(f"W0_{s}", [P, 2, F], FR) for s in ("hi", "lo")]
        W1 = [sb(f"W1_{s}", [P, 2, F], FR) for s in ("hi", "lo")]
        W2 = [sb(f"W2_{s}", [P, 2, F], FR) for s in ("hi", "lo")]
        WA = [sb(f"WA_{s}", [P, 2, FA], FR) for s in ("hi", "lo")]
        WB = [sb(f"WB_{s}", [P, 2, 2 * F], FR) for s in ("hi", "lo")]
        b0_bc = sb("b0_bc", [P, F])
        b2_bc = sb("b2_bc", [P, F])
        bk_bc = sb("bk_bc", [P, F])
        ident = sb("ident", [P, P])
        minus_half = sb("minus_half", [P, 4])
        eps = sb("eps", [P, 2])
        e_const = sb("e_const", [P, 1])
        ab_bc = sb("ab_bc", [P, 1])
        aw_sb = sb("aw_sb", [P, 2, 2])
        bv_sb = sb("bv_sb", [P, 2])

        xT_in = slots("xT_in", C)
        adj_in = slots("adj_in", C)
        adj3_in = slots("adj3_in", C)
        X0 = slots("X0_", C)
        X1 = slots("X1_", C)
        X2 = slots("X2_", C)
        X3 = slots("X3_", C)
        adj_hi, adj_lo = slots("adj_hi", C, FR), slots("adj_lo", C, FR)
        mix_hi, mix_lo = slots("mix_hi", 2 * FA, FR), slots("mix_lo", 2 * FA, FR)
        nod_hi, nod_lo = slots("nod_hi", C, FR), slots("nod_lo", C, FR)
        fea_hi, fea_lo = slots("fea_hi", C, FR), slots("fea_lo", C, FR)
        att_hi, att_lo = slots("att_hi", C, FR), slots("att_lo", C, FR)
        tmp = slots("tmp", C)
        P0 = slots("P0_", C)
        P1 = slots("P1_", C)
        stats = slots("stats", 12)
        mv = [slots(f"mv{l}_", 4) for l in range(4)]
        nmean = [slots(f"nmean{l}_", 2) for l in range(4)]
        powin = slots("powin", 4)
        rstd = slots("rstd", 4)
        rinv = slots("rinv", 2)
        absum = slots("absum", 2)
        mask = slots("mask", 2)
        logit = slots("logit", 6)

        ring = [ctx.enter_context(nc.psum_tensor(f"ring{g}", [P, C], FP)) for g in range(SLOTS)]
        pair = [ctx.enter_context(nc.psum_tensor(f"pair{i}", [P, 2, 512], FP)) for i in range(2)]

        xT_loaded, adj_loaded = sem4("xT_loaded"), sem4("adj_loaded")
        x_loaded, adj3_loaded = sem4("x_loaded"), sem4("adj3_loaded")
        
        s1_done, s2_done, s3_done, s4_done = sem("s1_done"), sem("s2_done"), sem4("s3_done"), sem("s4_done")
        s5_done, s6_done, s7_done = sem4("s5_done"), sem("s6_done"), sem4("s7_done")
        s8a_done, s8b_done, s9_done = sem("s8a_done"), sem("s8b_done"), sem("s9_done")
        s10_done, s11_done = sem("s10_done"), sem("s11_done")
        xT_hi_ready, xT_ready = sem("xT_hi_ready"), sem4("xT_ready")
        adj_hi_ready, adj_ready = sem("adj_hi_ready"), sem("adj_ready")
        xb_ready = sem("xb_ready")
        h_hi_ready, h_ready = sem("h_hi_ready"), sem("h_ready")
        deg_ready = sem("deg_ready")
        y_ready = [sem4(f"y{l}_ready") for l in range(4)]
        st_ready = [sem(f"st{l}_ready") for l in range(4)]
        mv_ready = [sem(f"mv{l}_ready") for l in range(4)]
        nm_ready = [sem(f"nm{l}_ready") for l in range(4)]
        pin_ready = [sem(f"pin{l}_ready") for l in range(4)]
        rstd_ready = [sem(f"rstd{l}_ready") for l in range(4)]
        rstdm_ready = sem("rstdm_ready")
        x_ready = [sem4(f"x{l}_ready") for l in range(4)]
        x1_hi_ready, x1_lo_ready = sem("x1_hi_ready"), sem("x1_lo_ready")
        absum_ready, mask_ready = sem("absum_ready"), sem("mask_ready")
        t1_hi_ready, t1_ready = sem("t1_hi_ready"), sem("t1_ready")
        xd_ready, xd_hi_ready, xd_lo_ready = sem("xd_ready"), sem("xd_hi_ready"), sem("xd_lo_ready")
        dsum_ready, dhi_ready, diag_ready = sem("dsum_ready"), sem("dhi_ready"), sem4("diag_ready")
        t2_hi_ready, t2_ready = sem("t2_hi_ready"), sem("t2_ready")
        z2_ready = sem("z2_ready")
        x3T_hi_ready, x3T_ready = sem("x3T_hi_ready"), sem("x3T_ready")
        logit_ready, P0_ready = sem("logit_ready"), sem("P0_ready")
        P1_ready, P2_hi_ready, P2_ready = sem("P1_ready"), sem("P2_hi_ready"), sem("P2_ready")
        sl_ready, e_ready, ex_ready = sem("sl_ready"), sem("e_ready"), sem("ex_ready")
        al_ready, al_hi_ready, al_lo_ready = sem4("al_ready"), sem("al_hi_ready"), sem("al_lo_ready")
        rinv0_ready, asum_ready, rinv3_ready = sem("rinv0_ready"), sem("asum_ready"), sem("rinv3_ready")
        Q_ready, Q_hi_ready, Q_lo_ready = sem("Q_ready"), sem("Q_hi_ready"), sem("Q_lo_ready")
        ring_free = sem4("ring_free")
        x3_free = sem4("x3_free")
        c_loaded, pool_c, bk_ready = sem("c_loaded"), sem("pool_c"), sem("bk_ready")
        u_done, u_ready, e_const_ready = sem("u_done"), sem("u_ready"), sem("e_const_ready")
        w_hi_ready, w_ready = sem("w_hi_ready"), sem("w_ready")

        def count(g, k):
            return SLOTS * k + g + 1

        def nodes(tile):
            return tile[:, :].rearrange("p (t f) -> p t f", t=2)

        def diag(tile):
            return tile[:, :].rearrange("p (j c) -> p j c", c=P)[:, 0:4:3, :]

        def mixed(tile):
            return tile[:, :].rearrange("p (t f) -> p t f", t=2)

        u_stage = P1[3][:, 0:4].rearrange("p (t c) -> p t c", t=2)
        staged = [(W0, slice(0, F), nodes(P0[0])), (W1, slice(0, F), nodes(P0[1])), (W2, slice(0, F), nodes(P0[2])),
                  (WA, slice(0, F), nodes(P0[3])), (WB, slice(0, F), nodes(P1[1])), (WB, slice(F, 2 * F), nodes(P1[2])),
                  (WA, slice(F, FA), u_stage)]
        bk_in = sb("bk_in", [P, 3 * F])
        c_loads = [(P0[0], w0), (P1[0], wvT), (aw_sb, aw), (bv_sb, bv), (P0[1], w1), (P0[2], w2), (P0[3], wk[0]), (P1[1], wk[1]),
                   (P1[2], wk[2])]
        C_LOADED = 16 * (len(c_loads) + 4)

        block = ctx.enter_context(nc.Block())

        @block.sync
        def _(sp):
            def graph(dram, g, k):
                return dram[bass.ds(k * SLOTS + g, 1)].rearrange("a p c -> (a p) c")

            def load_xT(g, kn):
                sp.wait_ge(xT_ready[g], kn)
                sp.dma_start(xT_in[g][:, :], graph(xT, g, kn)).then_inc(xT_loaded[g], 16)

            def load_x(g, kn):
                sp.wait_ge(x_ready[0][g], kn)
                sp.dma_start(X0[g][:, :], graph(x, g, kn)).then_inc(x_loaded[g], 16)

            def load_adj(g, kn):
                sp.wait_ge(diag_ready[g], kn)
                sp.dma_start(adj_in[g][:, :], graph(adjT, g, kn)).then_inc(adj_loaded[g], 16)

            def load_adj3(g, k):
                sp.wait_ge(al_ready[g], k)
                sp.dma_start(adj3_in[g][:, :], graph(adjT, g, k)).then_inc(adj3_loaded[g], 16)

            def store(g, k):
                sp.wait_ge(x_ready[3][g], k + 1)
                sp.dma_start(graph(out, g, k), X3[g][:, :]).then_inc(x3_free[g], 16)

            def iteration(k, left):
                if left >= 1:
                    for g in range(SLOTS):
                        load_adj(g, k + 1)
                if left >= 2:
                    for g in range(SLOTS):
                        load_xT(g, k + 2)
                    for g in range(SLOTS):
                        load_x(g, k + 2)
                if left >= 1:
                    for g in range(SLOTS):
                        load_adj3(g, k + 1)
                for g in range(SLOTS):
                    store(g, k)

            for load in (load_xT, load_adj, load_x, load_adj3):
                for g in range(SLOTS):
                    load(g, 0)
            for g in range(SLOTS):
                load_xT(g, 1)
            for g in range(SLOTS):
                load_x(g, 1)
            with sp.Fori(0, GROUPS - 2) as k:
                iteration(k, 2)
            iteration(GROUPS - 2, 1)
            iteration(GROUPS - 1, 0)
            for g in range(SLOTS):
                sp.wait_ge(x3_free[g], 16 * GROUPS + 16)

        @block.tensor
        def _(pe):
            mm = nc.tensor.matmul

            def product(dst, lhs, rhs):
                for i, o in enumerate(dst):
                    for t in range(2):
                        mm(o, lhs(1, t, i), rhs(0, t), start=t == 0, stop=False)
                        mm(o, lhs(0, t, i), rhs(1, t), start=False, stop=False)
                        last = mm(o, lhs(0, t, i), rhs(0, t), start=False, stop=t == 1)
                return last

            def cols(parts, g):
                return lambda s, t, i: parts[s][g][:, t * N + i * P:t * N + (i + 1) * P]

            def rows(parts, g):
                return lambda s, t: parts[s][g][:, t * N:(t + 1) * N]

            adj, nod, fea, att, mix = ((adj_hi, adj_lo), (nod_hi, nod_lo), (fea_hi, fea_lo), (att_hi, att_lo), (mix_hi, mix_lo))

            def halves(g):
                return [ring[g][:, 0:N], ring[g][:, N:2 * N]]

            def s1(g, kn):
                pe.wait_ge(xT_ready[g], kn + 1)
                pe.wait_ge(y_ready[1][g], kn)
                product(halves(g), cols(att, g), lambda s, t: W0[s][:, t, :]).then_inc(s1_done, 1)

            def s2(g, kn):
                pe.wait_ge(h_ready, count(g, kn))
                pe.wait_ge(adj_ready, count(g, kn))
                if g >= 2:
                    pe.wait_ge(y_ready[0][g - 2], kn + 1)
                product([pair[g % 2][:, i, 0:FA] for i in range(2)], cols(adj, g),
                        lambda s, t: mixed(mix[s][g])[:, t, :]).then_inc(s2_done, 1)

            def s3(g, k):
                pe.wait_ge(x1_lo_ready, count(g, k))
                pe.wait_ge(ring_free[g], k + 1)
                product(halves(g), cols(nod, g), rows(adj, g)).then_inc(s3_done[g], 1)

            def s4(g, k):
                pe.wait_ge(t1_ready, count(g, k))
                product(halves(g), cols(fea, g), lambda s, t: W1[s][:, t, :]).then_inc(s4_done, 1)

            def s5(g, k, last):
                pe.wait_ge(xd_lo_ready, count(g, k))
                pe.wait_ge(diag_ready[g], k + 1)
                if not last:
                    pe.wait_ge(h_ready, count(g, k + 1))
                product(halves(g), cols(nod, g), rows(adj, g)).then_inc(s5_done[g], 1)

            def s6(g, k):
                pe.wait_ge(t2_ready, count(g, k))
                product(halves(g), cols(fea, g), lambda s, t: W2[s][:, t, :]).then_inc(s6_done, 1)

            def s7(g, k):
                pe.wait_ge(x_ready[2][g], k + 1)
                for f in range(2):
                    for t in range(2):
                        last = nc.tensor.transpose(ring[g][:, f * N + t * P:f * N + (t + 1) * P],
                                                   nodes(X3[g])[:, t, f * P:(f + 1) * P], ident[:, :])
                last.then_inc(s7_done[g], 1)

            def s8a(g, k, last):
                pe.wait_ge(x3T_ready, count(g, k))
                if g >= 1:
                    pe.wait_ge(P0_ready, count(g - 1, k))
                elif not last:
                    pe.wait_ge(y_ready[0][2], k + 2)
                product([pair[0][:, i, 0:FA] for i in range(2)], cols(fea, g),
                        lambda s, t: WA[s][:, t, :]).then_inc(s8a_done, 1)

            def s8b(g, k, last):
                if g >= 1:
                    pe.wait_ge(P2_ready, count(g - 1, k))
                elif not last:
                    pe.wait_ge(y_ready[0][3], k + 2)
                product([pair[1][:, i, :] for i in range(2)], cols(fea, g),
                        lambda s, t: WB[s][:, t, :]).then_inc(s8b_done, 1)

            def s9(g, k):
                pe.wait_ge(logit_ready, count(g, k))
                for t in range(2):
                    last = nc.tensor.transpose(ring[g][:, t * P:(t + 1) * P],
                                               logit[g][:, 4 + t:5 + t].to_broadcast([P, P]), ident[:, :])
                last.then_inc(s9_done, 1)

            def s10(g, k):
                pe.wait_ge(al_lo_ready, count(g, k))
                if g == 0:
                    pe.wait_ge(P0_ready, count(SLOTS - 1, k))
                elif g == 1:
                    pe.wait_ge(P2_ready, count(SLOTS - 1, k))
                else:
                    pe.wait_ge(Q_ready, count(g - 2, k))
                product([pair[g % 2][:, i, 0:FA] for i in range(2)], cols(att, g),
                        lambda s, t: mixed(mix[s][g])[:, t, :]).then_inc(s10_done, 1)

            def s11(g, k):
                pe.wait_ge(Q_lo_ready, count(g, k))
                product(halves(g), cols(att, g), rows(fea, g)).then_inc(s11_done, 1)

            def iteration(k, last):
                for g in range(SLOTS):
                    s3(g, k)
                for g in range(SLOTS):
                    s4(g, k)
                if not last:
                    for g in range(SLOTS):
                        s1(g, k + 1)
                for g in range(SLOTS):
                    s5(g, k, last)
                for g in range(SLOTS):
                    s6(g, k)
                if not last:
                    for g in range(SLOTS):
                        s2(g, k + 1)
                for g in range(SLOTS):
                    s7(g, k)
                for g in range(SLOTS):
                    s8a(g, k, last)
                    s8b(g, k, last)
                    s9(g, k)
                for g in range(SLOTS):
                    s10(g, k)
                for g in range(SLOTS):
                    s11(g, k)

            pe.wait_ge(c_loaded, C_LOADED)
            for f in range(2):
                for t in range(2):
                    mm(ring[0][:, 2 * f:2 * f + 2], P1[0][:, t * F + f * P:t * F + (f + 1) * P], aw_sb[:, t, :],
                       start=t == 0, stop=t == 1)
            for t in range(2):
                last = mm(ring[0][:, 4:6], bv_sb[:, t:t + 1].to_broadcast([P, P]), aw_sb[:, t, :], start=t == 0, stop=t == 1)
            last.then_inc(u_done, 1)
            pe.wait_ge(w_ready, 1)
            for g in range(SLOTS):
                s1(g, 0)
            for g in range(SLOTS):
                s2(g, 0)
            with pe.Fori(0, GROUPS - 1) as k:
                iteration(k, False)
            iteration(GROUPS - 1, True)

        @block.scalar
        def _(act):
            def copy(dst, src):
                return nc.scalar.activation(dst, src, ACT.Copy)

            def xT_split(g, kn):
                act.wait_ge(xT_loaded[g], 16 * kn + 16)
                copy(att_hi[g][:, :], xT_in[g][:, :]).then_inc(xT_hi_ready, 1)

            def h_hi(g, kn):
                act.wait_ge(s1_done, count(g, kn))
                copy(mixed(mix_hi[g])[:, :, 0:F], nodes(ring[g])).then_inc(h_hi_ready, 1)

            def x1_split(g, kn):
                act.wait_ge(x_ready[0][g], kn + 1)
                copy(nod_hi[g][:, :], X1[g][:, :]).then_inc(x1_hi_ready, 1)
                for t in range(2):
                    last = nc.scalar.activation(P1[g][:, t * F:(t + 1) * F], nodes(X1[g])[:, t, :], ACT.Abs,
                                                accum_out=absum[g][:, t:t + 1])
                last.then_inc(absum_ready, 1)

            def adj_split(g, kn):
                act.wait_ge(adj_loaded[g], 16 * kn + 16)
                act.wait_ge(s5_done[g], kn)
                copy(adj_hi[g][:, :], adj_in[g][:, :]).then_inc(adj_hi_ready, 1)

            def from_ring(g, done, k, dst, ready):
                act.wait_ge(done[g], k + 1)
                copy(dst[g][:, :], ring[g][:, :]).then_inc(ready, 1)

            def xd_hi(g, k):
                act.wait_ge(xd_ready, count(g, k))
                copy(nod_hi[g][:, :], tmp[g][:, :]).then_inc(xd_hi_ready, 1)

            def diag_hi(g, k):
                act.wait_ge(dsum_ready, count(g, k))
                act.wait_ge(s3_done[g], k + 1)
                copy(diag(adj_hi[g]), diag(adj_in[g])).then_inc(dhi_ready, 1)

            def p12(g, k, last):
                act.wait_ge(s8b_done, count(g, k))
                copy(mixed(mix_hi[g])[:, :, 0:F], pair[1][:, :, F:2 * F]).then_inc(P2_hi_ready, 1)
                act.wait_ge(absum_ready, count(g, k if last else k + 1))
                copy(nodes(P1[g]), pair[1][:, :, 0:F]).then_inc(P1_ready, 1)

            def slope(g, k):
                act.wait_ge(s9_done, count(g, k))
                act.wait_ge(logit_ready, count(g, k))
                for t in range(2):
                    last = nc.scalar.activation(tmp[g][:, t * N:(t + 1) * N], ring[g][:, 0:N], ACT.Identity,
                                                scale=0.2, bias=logit[g][:, 2 + t:3 + t])
                last.then_inc(sl_ready, 1)

            def exp(g, k):
                act.wait_ge(e_ready, count(g, k))
                nc.scalar.activation(tmp[g][:, :], tmp[g][:, :], ACT.Exp).then_inc(ex_ready, 1)

            def alpha_hi(g, k):
                act.wait_ge(al_ready[g], k + 1)
                copy(att_hi[g][:, :], tmp[g][:, :]).then_inc(al_hi_ready, 1)

            def q_hi(g, k):
                act.wait_ge(Q_ready, count(g, k))
                copy(fea_hi[g][:, :], P1[g][:, :]).then_inc(Q_hi_ready, 1)

            def iteration(k, last):
                for g in range(SLOTS):
                    from_ring(g, s3_done, k, fea_hi, t1_hi_ready)
                    diag_hi(g, k)
                if not last:
                    for g in range(SLOTS):
                        xT_split(g, k + 1)
                for i in range(SLOTS + 2):
                    if i < SLOTS and not last:
                        h_hi(i, k + 1)
                    if i < SLOTS:
                        xd_hi(i, k)
                for g in range(SLOTS):
                    from_ring(g, s5_done, k, fea_hi, t2_hi_ready)
                    if not last:
                        adj_split(g, k + 1)
                for g in range(SLOTS):
                    from_ring(g, s7_done, k, fea_hi, x3T_hi_ready)
                for i in range(SLOTS + 1):
                    if i < SLOTS:
                        if not last:
                            x1_split(i, k + 1)
                        p12(i, k, last)
                        slope(i, k)
                    if i >= 1:
                        exp(i - 1, k)
                for g in range(SLOTS):
                    alpha_hi(g, k)
                for g in range(SLOTS):
                    q_hi(g, k)

            for tile, dram in c_loads:
                act.dma_start(tile[:, :], dram).then_inc(c_loaded, 16)
            act.dma_start(b0_bc[:, :], b0.to_broadcast([P, F])).then_inc(c_loaded, 16)
            act.dma_start(b2_bc[:, :], b2.to_broadcast([P, F])).then_inc(c_loaded, 16)
            act.dma_start(bk_in[:, :], bk.to_broadcast([P, 3 * F])).then_inc(c_loaded, 16)
            act.dma_start(ab_bc[:, :], ab.to_broadcast([P, 1])).then_inc(c_loaded, 16)
            act.wait_ge(c_loaded, C_LOADED)
            act.wait_ge(u_ready, 1)
            for w, columns, stage in staged:
                last = copy(w[0][:, :, columns], stage)
            last.then_inc(w_hi_ready, 1)
            for g in range(SLOTS):
                xT_split(g, 0)
                adj_split(g, 0)
            for g in range(SLOTS):
                h_hi(g, 0)
            for g in range(SLOTS):
                x1_split(g, 0)
            with act.Fori(0, GROUPS - 1) as k:
                iteration(k, False)
            iteration(GROUPS - 1, True)

        @block.gpsimd
        def _(pool):
            ts, tt = nc.gpsimd.tensor_scalar, nc.gpsimd.tensor_tensor

            def xT_lo(g, kn):
                pool.wait_ge(xT_hi_ready, count(g, kn))
                tt(att_lo[g][:, :], xT_in[g][:, :], att_hi[g][:, :], ALU.subtract).then_inc(xT_ready[g], 1)

            def x_bias(g, kn):
                pool.wait_ge(x_loaded[g], 16 * kn + 16)
                tt(nodes(X0[g]), nodes(X0[g]), b0_bc[:, :].unsqueeze(1).to_broadcast([P, 2, F]), ALU.add).then_inc(xb_ready, 1)

            def adj_low(g, kn):
                pool.wait_ge(adj_hi_ready, count(g, kn))
                tt(adj_lo[g][:, :], adj_in[g][:, :], adj_hi[g][:, :], ALU.subtract).then_inc(adj_ready, 1)

            def x1_lo(g, kn):
                pool.wait_ge(x1_hi_ready, count(g, kn))
                tt(nod_lo[g][:, :], X1[g][:, :], nod_hi[g][:, :], ALU.subtract).then_inc(x1_lo_ready, 1)

            def norm(l, g, k, src, dst):
                n = 4 if l == 0 else 2
                pool.wait_ge(mv_ready[l], count(g, k))
                tt(powin[g][:, 0:2], mv[l][g][:, 1:4:2], eps[:, :], ALU.add).then_inc(pin_ready[l], 1)
                pool.wait_ge(pin_ready[l], count(g, k))
                if l == 0:
                    pool.wait_ge(deg_ready, count(g, k))
                if l == 2:
                    pool.wait_ge(x3_free[g], 16 * k + 16)
                tt(rstd[g][:, 0:n], powin[g][:, 0:n], minus_half[:, 0:n], ALU.pow).then_inc(rstd_ready[l], 1)
                if l == 1:
                    pool.wait_ge(rstd_ready[l], count(g, k))
                    pool.wait_ge(mask_ready, count(g, k))
                    tt(rstd[g][:, 0:2], rstd[g][:, 0:2], mask[g][:, :], ALU.mult).then_inc(rstdm_ready, 1)
                pool.wait_ge(pool_c, 3)
                pool.wait_ge(rstdm_ready if l == 1 else rstd_ready[l], count(g, k))
                pool.wait_ge(nm_ready[l], count(g, k))
                for t in range(2):
                    last = ts(nodes(dst[g])[:, t, :], nodes(src[g])[:, t, :], nmean[l][g][:, t:t + 1], rstd[g][:, t:t + 1],
                              ALU.add, ALU.mult)
                last.then_inc(x_ready[l][g], 1)

            def diag_sum(g, k):
                pool.wait_ge(adj_ready, count(g, k))
                ident2 = ident[:, :].unsqueeze(1).to_broadcast([P, 2, P])
                tt(diag(adj_in[g]), diag(adj_in[g]), ident2, ALU.add).then_inc(dsum_ready, 1)

            def iteration(k, last):
                for g in range(SLOTS):
                    if not last:
                        xT_lo(g, k + 1)
                for g in range(SLOTS):
                    norm(1, g, k, X1, X2)
                    if not last:
                        x_bias(g, k + 1)
                for g in range(SLOTS):
                    if not last:
                        adj_low(g, k + 1)
                for g in range(SLOTS):
                    norm(2, g, k, X2, X3)
                if not last:
                    for i in range(SLOTS + 1):
                        if i < SLOTS:
                            norm(0, i, k + 1, X0, X1)
                        if i >= 1:
                            x1_lo(i - 1, k + 1)
                    for g in range(SLOTS):
                        diag_sum(g, k + 1)
                for g in range(SLOTS):
                    norm(3, g, k, X3, X3)

            pool.memset(ident[:, :], 0.0).then_inc(pool_c, 1)
            pool.wait_ge(pool_c, 1)
            pool.affine_select(out=ident[:, :], in_=ident[:, :], compare_op=ALU.not_equal, fill=1.0, base=0,
                               pattern=[[-1, P]], channel_multiplier=1).then_inc(pool_c, 1)
            pool.memset(minus_half[:, :], -0.5)
            pool.memset(eps[:, :], EPS).then_inc(pool_c, 1)
            pool.wait_ge(pool_c, 3)
            pool.wait_ge(c_loaded, C_LOADED)
            tt(bk_bc[:, :], bk_in[:, 0:F], bk_in[:, F:2 * F], ALU.add).then_inc(pool_c, 1)
            pool.wait_ge(pool_c, 4)
            tt(bk_bc[:, :], bk_bc[:, :], bk_in[:, 2 * F:3 * F], ALU.add).then_inc(bk_ready, 1)
            for g in range(SLOTS):
                xT_lo(g, 0)
                adj_low(g, 0)
            for g in range(SLOTS):
                x_bias(g, 0)
            for i in range(SLOTS + 1):
                if i < SLOTS:
                    norm(0, i, 0, X0, X1)
                if i >= 1:
                    x1_lo(i - 1, 0)
            for g in range(SLOTS):
                diag_sum(g, 0)
            with pool.Fori(0, GROUPS - 1) as k:
                iteration(k, False)
            iteration(GROUPS - 1, True)

        @block.vector
        def _(dve):
            ts, tt, stt = nc.vector.tensor_scalar, nc.vector.tensor_tensor, nc.vector.scalar_tensor_tensor

            def from_ring(g, hi_ready, k, hi, lo, ready):
                dve.wait_ge(hi_ready, count(g, k))
                tt(lo[g][:, :], ring[g][:, :], hi[g][:, :], ALU.subtract).then_inc(ready, 1)

            def h_lo(g, kn):
                dve.wait_ge(h_hi_ready, count(g, kn))
                tt(mixed(mix_lo[g])[:, :, 0:F], nodes(ring[g]), mixed(mix_hi[g])[:, :, 0:F], ALU.subtract).then_inc(h_ready, 1)

            def statistics(l, g, k, y):
                dve.wait_ge(y_ready[l][g], k + 1)
                for t in range(2):
                    last = nc.vector.bn_stats(stats[g][:, 6 * t:6 * t + 6], nodes(y[g])[:, t, :])
                last.then_inc(st_ready[l], 1)

            def moments(l, g, k):
                dve.wait_ge(e_const_ready, 2)
                dve.wait_ge(st_ready[l], count(g, k))
                for t in range(2):
                    last = nc.vector.bn_aggr(mv[l][g][:, 2 * t:2 * t + 2], stats[g][:, 6 * t:6 * t + 6])
                last.then_inc(mv_ready[l], 1)
                dve.wait_ge(mv_ready[l], count(g, k))
                ts(nmean[l][g][:, :], mv[l][g][:, 0:4:2], -1.0, None, ALU.mult).then_inc(nm_ready[l], 1)

            def y0(g, kn):
                dve.wait_ge(s2_done, count(g, kn))
                sums = pair[g % 2][:, :, F]
                nc.vector.reciprocal(rinv[g][:, :], sums).then_inc(rinv0_ready, 1)
                ts(powin[g][:, 2:4], sums, 1.0, None, ALU.add).then_inc(deg_ready, 1)
                dve.wait_ge(rinv0_ready, count(g, kn))
                dve.wait_ge(xb_ready, count(g, kn))
                for t in range(2):
                    last = stt(nodes(X0[g])[:, t, :], pair[g % 2][:, t, 0:F], rinv[g][:, t:t + 1], nodes(X0[g])[:, t, :],
                               ALU.mult, ALU.add)
                last.then_inc(y_ready[0][g], 1)

            def layer1_mask(g, kn):
                dve.wait_ge(absum_ready, count(g, kn))
                ts(mask[g][:, :], absum[g][:, :], 0.0, None, ALU.is_gt).then_inc(mask_ready, 1)

            def y1(g, k):
                dve.wait_ge(s4_done, count(g, k))
                stt(X1[g][:, :], ring[g][:, :], 0.0, X1[g][:, :], ALU.max, ALU.add).then_inc(y_ready[1][g], 1)

            def xd(g, k):
                dve.wait_ge(x_ready[1][g], k + 1)
                for t in range(2):
                    last = ts(tmp[g][:, t * F:(t + 1) * F], nodes(X2[g])[:, t, :], rstd[g][:, 2 + t:3 + t], None, ALU.mult)
                last.then_inc(xd_ready, 1)

            def xd_lo(g, k):
                dve.wait_ge(xd_hi_ready, count(g, k))
                tt(nod_lo[g][:, :], tmp[g][:, :], nod_hi[g][:, :], ALU.subtract).then_inc(xd_lo_ready, 1)

            def diag_lo(g, k):
                dve.wait_ge(dhi_ready, count(g, k))
                tt(diag(adj_lo[g]), diag(adj_in[g]), diag(adj_hi[g]), ALU.subtract).then_inc(diag_ready[g], 1)

            def y2(g, k):
                dve.wait_ge(s6_done, count(g, k))
                for t in range(2):
                    last = stt(tmp[g][:, t * F:(t + 1) * F], ring[g][:, t * N:(t + 1) * N], rstd[g][:, 2 + t:3 + t], b2_bc[:, :],
                               ALU.mult, ALU.add)
                last.then_inc(z2_ready, 1)

            def y2b(g, k):
                dve.wait_ge(z2_ready, count(g, k))
                stt(X2[g][:, :], tmp[g][:, :], 0.0, X2[g][:, :], ALU.max, ALU.add).then_inc(y_ready[2][g], 1)

            def p0(g, k):
                dve.wait_ge(s8a_done, count(g, k))
                ts(logit[g][:, 0:2], pair[0][:, :, F], e_const[:, 0:1], None, ALU.add)
                ts(logit[g][:, 2:4], pair[0][:, :, F], e_const[:, 0:1], 0.2, ALU.add, ALU.mult)
                nc.vector.tensor_copy(logit[g][:, 4:6], pair[0][:, :, F + 1]).then_inc(logit_ready, 1)
                tt(nodes(P0[g]), pair[0][:, :, 0:F], bk_bc[:, :].unsqueeze(1).to_broadcast([P, 2, F]), ALU.add).then_inc(P0_ready, 1)

            def p2_lo(g, k):
                dve.wait_ge(P2_hi_ready, count(g, k))
                dve.wait_ge(P1_ready, count(g, k))
                tt(mixed(mix_lo[g])[:, :, 0:F], pair[1][:, :, F:2 * F], mixed(mix_hi[g])[:, :, 0:F], ALU.subtract).then_inc(P2_ready, 1)

            def leaky(g, k):
                dve.wait_ge(sl_ready, count(g, k))
                for t in range(2):
                    last = stt(tmp[g][:, t * N:(t + 1) * N], ring[g][:, 0:N], logit[g][:, t:t + 1], tmp[g][:, t * N:(t + 1) * N],
                               ALU.add, ALU.max)
                last.then_inc(e_ready, 1)

            def alpha(g, k):
                dve.wait_ge(ex_ready, count(g, k))
                dve.wait_ge(adj3_loaded[g], 16 * k + 16)
                tt(tmp[g][:, :], tmp[g][:, :], adj3_in[g][:, :], ALU.mult).then_inc(al_ready[g], 1)

            def alpha_lo(g, k):
                dve.wait_ge(al_hi_ready, count(g, k))
                tt(att_lo[g][:, :], tmp[g][:, :], att_hi[g][:, :], ALU.subtract).then_inc(al_lo_ready, 1)

            def q(g, k):
                dve.wait_ge(s10_done, count(g, k))
                ts(rinv[g][:, :], pair[g % 2][:, :, F], 1e-12, None, ALU.add).then_inc(asum_ready, 1)
                dve.wait_ge(asum_ready, count(g, k))
                nc.vector.reciprocal(rinv[g][:, :], rinv[g][:, :]).then_inc(rinv3_ready, 1)
                dve.wait_ge(rinv3_ready, count(g, k))
                for t in range(2):
                    last = stt(nodes(P1[g])[:, t, :], pair[g % 2][:, t, 0:F], rinv[g][:, t:t + 1], nodes(P1[g])[:, t, :],
                               ALU.mult, ALU.add)
                last.then_inc(Q_ready, 1)

            def q_lo(g, k):
                dve.wait_ge(Q_hi_ready, count(g, k))
                tt(fea_lo[g][:, :], P1[g][:, :], fea_hi[g][:, :], ALU.subtract).then_inc(Q_lo_ready, 1)

            def z3(g, k):
                dve.wait_ge(s11_done, count(g, k))
                for t in range(2):
                    last = stt(nodes(P0[g])[:, t, :], ring[g][:, t * F:(t + 1) * F], rinv[g][:, t:t + 1], nodes(P0[g])[:, t, :],
                               ALU.mult, ALU.add)
                last.then_inc(ring_free[g], 1)

            def y3(g, k):
                dve.wait_ge(ring_free[g], k + 2)
                stt(X3[g][:, :], P0[g][:, :], 0.0, X3[g][:, :], ALU.max, ALU.add).then_inc(y_ready[3][g], 1)

            def iteration(k, last):
                for g in range(SLOTS):
                    from_ring(g, t1_hi_ready, k, fea_hi, fea_lo, t1_ready)
                    diag_lo(g, k)
                for i in range(SLOTS + 2):
                    if i < SLOTS:
                        y1(i, k)
                        statistics(1, i, k, X1)
                        moments(1, i, k)
                    if 0 <= i - 2:
                        if not last:
                            h_lo(i - 2, k + 1)
                        xd(i - 2, k)
                        xd_lo(i - 2, k)
                for g in range(SLOTS):
                    from_ring(g, t2_hi_ready, k, fea_hi, fea_lo, t2_ready)
                for g in range(SLOTS):
                    y2(g, k)
                    y2b(g, k)
                    statistics(2, g, k, X2)
                    moments(2, g, k)
                if not last:
                    for g in range(SLOTS):
                        y0(g, k + 1)
                        statistics(0, g, k + 1, X0)
                        moments(0, g, k + 1)
                for g in range(SLOTS):
                    from_ring(g, x3T_hi_ready, k, fea_hi, fea_lo, x3T_ready)
                for i in range(SLOTS + 1):
                    if i < SLOTS:
                        p0(i, k)
                        if not last:
                            layer1_mask(i, k + 1)
                        p2_lo(i, k)
                        leaky(i, k)
                    if i >= 1:
                        alpha(i - 1, k)
                for g in range(SLOTS):
                    alpha_lo(g, k)
                for i in range(SLOTS + 1):
                    if i < SLOTS:
                        q(i, k)
                    if i >= 1:
                        q_lo(i - 1, k)
                for g in range(SLOTS):
                    z3(g, k)
                    y3(g, k)
                    statistics(3, g, k, X3)
                    moments(3, g, k)

            for g in range(SLOTS):
                nc.vector.memset(mixed(mix_hi[g])[:, :, F:FA].bitcast(FP), 1.0).then_inc(ring_free[g], 1)
                nc.vector.memset(mixed(mix_lo[g])[:, :, F:FA].bitcast(FP), 0.0).then_inc(x3_free[g], 16)
            dve.wait_ge(u_done, 1)
            dve.wait_ge(c_loaded, C_LOADED)
            nc.vector.tensor_copy(u_stage, ring[0][:, 0:4].rearrange("p (t c) -> p t c", t=2)).then_inc(u_ready, 1)
            ts(e_const[:, :], ring[0][:, 4:5], ab_bc[:, 0:1], None, ALU.add).then_inc(e_const_ready, 1)
            dve.wait_ge(e_const_ready, 1)
            tt(e_const[:, :], ring[0][:, 5:6], e_const[:, :], ALU.add).then_inc(e_const_ready, 1)
            dve.wait_ge(e_const_ready, 2)
            dve.wait_ge(bk_ready, 1)
            dve.wait_ge(w_hi_ready, 1)
            for w, columns, stage in staged:
                last = tt(w[1][:, :, columns], stage, w[0][:, :, columns], ALU.subtract)
            last.then_inc(w_ready, 1)
            for g in range(SLOTS):
                h_lo(g, 0)
            for g in range(SLOTS):
                y0(g, 0)
                statistics(0, g, 0, X0)
                moments(0, g, 0)
            for g in range(SLOTS):
                layer1_mask(g, 0)
            with dve.Fori(0, GROUPS - 1) as k:
                iteration(k, False)
            iteration(GROUPS - 1, True)


def kernel(x, adj, L0_gnn_W, L0_gnn_b, L1_gnn_kernel, L2_gnn_kernel, L2_gnn_bias, L3_gnn_Wv, L3_gnn_bv, L3_gnn_aw,
           L3_gnn_ab, L3_gnn_Wk, L3_gnn_bk):
    import numpy as np
    import concourse.bacc as bacc
    from concourse.bass_utils import run_bass_kernel_spmd

    B, N, F = x.shape
    C = 2 * N

    def by_feature(w):
        w = np.asarray(w)
        return w.reshape(2, P, -1).transpose(1, 0, 2).reshape(P, -1)

    def nodes_last(a):
        return a.reshape(B, -1, P, 2).transpose(0, 1, 3, 2).reshape(B, -1, N)

    x, adj = np.asarray(x), np.asarray(adj)
    xT = nodes_last(x.transpose(0, 2, 1)).reshape(B, 2, P, N).transpose(0, 2, 1, 3).reshape(B, P, C)
    adjT = nodes_last(adj.transpose(0, 2, 1)).reshape(B, P, C)
    data = {
        "x": x.reshape(B, P, C), "xT": xT, "adjT": adjT,
        "w0": by_feature(L0_gnn_W), "w1": by_feature(L1_gnn_kernel), "w2": by_feature(L2_gnn_kernel),
        "wk": np.stack([by_feature(w) for w in np.asarray(L3_gnn_Wk)]),
        "wvT": by_feature(np.asarray(L3_gnn_Wv).T),
        "aw": by_feature(np.asarray(L3_gnn_aw).reshape(2, F).T), "bv": by_feature(np.asarray(L3_gnn_bv).reshape(F, 1)),
        "ab": np.asarray(L3_gnn_ab).reshape(1, 1), "b0": np.asarray(L0_gnn_b).reshape(1, F),
        "b2": np.asarray(L2_gnn_bias).reshape(1, F), "bk": np.asarray(L3_gnn_bk).reshape(1, 3 * F),
    }
    data = {name: np.ascontiguousarray(a) for name, a in data.items()}
    nc = bacc.Bacc("TRN2", target_bir_lowering=False, num_devices=1)
    drams = {name: nc.dram_tensor(f"{name}_dram", a.shape, mybir.dt.from_np(a.dtype), kind="ExternalInput").ap()
             for name, a in data.items()}
    out = nc.dram_tensor("out_dram", (B, P, C), FP, kind="ExternalOutput").ap()
    build(nc, out=out, **drams)
    result = run_bass_kernel_spmd(nc, [{f"{name}_dram": a for name, a in data.items()}], core_ids=[0])
    return result.results[0]["out_dram"].reshape(B, N, F)
```

```python
from contextlib import ExitStack

import concourse.bass as bass
from concourse import mybir

P = 128
SLOTS = 4
EPS = 1e-5
FP = mybir.dt.float32
FR = mybir.dt.float32r
ALU = mybir.AluOpType
ACT = mybir.ActivationFunctionType


def build(nc, x, xT, adjT, w0, w1, w2, wk, wvT, aw, bv, ab, b0, b2, bk, out):
    B = x.shape[0]
    N = x.shape[2] // 2
    F = N
    GROUPS = B // SLOTS
    C = 2 * N
    FA = F + 2

    with ExitStack() as ctx:
        def sb(name, shape, dt=FP):
            return ctx.enter_context(nc.sbuf_tensor(name, shape, dt))

        def sem(name):
            return ctx.enter_context(nc.semaphore(name))

        def sem4(name):
            return [sem(f"{name}{g}") for g in range(SLOTS)]

        def slots(name, cols, dt=FP):
            return [sb(f"{name}{g}", [P, cols], dt) for g in range(SLOTS)]

        W0 = sb("W0", [P, 2, F])
        W1 = [sb(f"W1_{s}", [P, 2, F], FR) for s in ("hi", "lo")]
        W2 = [sb(f"W2_{s}", [P, 2, F], FR) for s in ("hi", "lo")]
        WA = [sb(f"WA_{s}", [P, 2, FA], FR) for s in ("hi", "lo")]
        WB = [sb(f"WB_{s}", [P, 2, 2 * F], FR) for s in ("hi", "lo")]
        b0_bc = sb("b0_bc", [P, F])
        b2_bc = sb("b2_bc", [P, F])
        bk_bc = sb("bk_bc", [P, F])
        ident = sb("ident", [P, P])
        minus_half = sb("minus_half", [P, 4])
        eps = sb("eps", [P, 2])
        e_const = sb("e_const", [P, 1])
        ab_bc = sb("ab_bc", [P, 1])
        aw_sb = sb("aw_sb", [P, 2, 2])
        bv_sb = sb("bv_sb", [P, 2])

        xT_in = slots("xT_in", C)
        adj_in = slots("adj_in", C)
        adj3_in = slots("adj3_in", C)
        X0 = slots("X0_", C)
        X1 = slots("X1_", C)
        X2 = slots("X2_", C)
        X3 = slots("X3_", C)
        adj_hi, adj_lo = slots("adj_hi", C, FR), slots("adj_lo", C, FR)
        h_hi, h_lo = slots("h_hi", 2 * FA, FR), slots("h_lo", 2 * FA, FR)
        P2 = slots("P2_", 2 * FA)
        nod_hi, nod_lo = slots("nod_hi", C, FR), slots("nod_lo", C, FR)
        fea_hi, fea_lo = slots("fea_hi", C, FR), slots("fea_lo", C, FR)
        tmp = slots("tmp", C)
        P0 = slots("P0_", C)
        P1 = slots("P1_", C)
        stats = [slots(f"stats{l}_", 12) for l in range(4)]
        mv = [slots(f"mv{l}_", 4) for l in range(4)]
        nmean = [slots(f"nmean{l}_", 2) for l in range(4)]
        powin = [slots(f"powin{l}_", 4) for l in range(4)]
        rstd = [slots(f"rstd{l}_", 4) for l in range(4)]
        nmr = {l: slots(f"nmr{l}_", 2) for l in (2, 3)}
        rinv = slots("rinv", 2)
        absum = slots("absum", 2)
        mask = slots("mask", 2)
        logit = slots("logit", 6)

        X = [X0, X1, X2, X3]
        ring = [ctx.enter_context(nc.psum_tensor(f"ring{g}", [P, C], FP)) for g in range(SLOTS)]
        pair = [ctx.enter_context(nc.psum_tensor(f"pair{i}", [P, 2, 512], FP)) for i in range(2)]

        xT_loaded, adj_loaded = sem4("xT_loaded"), sem4("adj_loaded")
        x_loaded, adj3_loaded = sem4("x_loaded"), sem4("adj3_loaded")
        
        s1_done, s2_done, s3_done, s4_done = sem("s1_done"), sem("s2_done"), sem4("s3_done"), sem("s4_done")
        s5_done, s6_done, s7_done = sem4("s5_done"), sem("s6_done"), sem4("s7_done")
        s8a_done, s8b_done, s9_done = sem("s8a_done"), sem("s8b_done"), sem("s9_done")
        s10_done, s11_done = sem("s10_done"), sem("s11_done")
        adj_hi_ready, adj_ready = sem("adj_hi_ready"), sem("adj_ready")
        xb_ready = sem("xb_ready")
        h_hi_ready, h_ready = sem("h_hi_ready"), sem("h_ready")
        deg_ready, z0_ready = sem("deg_ready"), sem("z0_ready")
        y_ready = [sem4(f"y{l}_ready") for l in range(4)]
        st_ready = [sem(f"st{l}_ready") for l in range(4)]
        mv_ready = [sem(f"mv{l}_ready") for l in range(4)]
        nm_ready = [sem(f"nm{l}_ready") for l in range(4)]
        pin_ready = [sem(f"pin{l}_ready") for l in range(4)]
        rstd_ready = [sem(f"rstd{l}_ready") for l in range(4)]
        rstdm_ready = sem("rstdm_ready")
        nmr_ready = {l: sem(f"nmr{l}_ready") for l in (2, 3)}
        x_ready = [sem4(f"x{l}_ready") for l in range(4)]
        x1_hi_ready, x1_lo_ready = sem("x1_hi_ready"), sem("x1_lo_ready")
        absum_ready, mask_ready = sem4("absum_ready"), sem("mask_ready")
        t1_hi_ready, t1_ready = sem("t1_hi_ready"), sem("t1_ready")
        xd_hi_ready, xd_lo_ready = sem("xd_hi_ready"), sem("xd_lo_ready")
        dsum_ready, dhi_ready, diag_ready = sem("dsum_ready"), sem("dhi_ready"), sem4("diag_ready")
        t2_hi_ready, t2_ready = sem("t2_hi_ready"), sem("t2_ready")
        z2_ready = sem("z2_ready")
        x3T_hi_ready, x3T_ready = sem("x3T_hi_ready"), sem("x3T_ready")
        logit_ready, P0_ready = sem("logit_ready"), sem("P0_ready")
        P12_ready, Q_ready = sem("P12_ready"), sem("Q_ready")
        sl_ready, e_ready, ex_ready, al_ready = sem("sl_ready"), sem("e_ready"), sem("ex_ready"), sem4("al_ready")
        rinv0_ready, asum_ready, rinv3_ready = sem("rinv0_ready"), sem("asum_ready"), sem("rinv3_ready")
        z3_ready = sem("z3_ready")
        x3_free = sem4("x3_free")
        c_loaded, pool_c, bk_ready = sem("c_loaded"), sem("pool_c"), sem("bk_ready")
        u_done, u_ready, e_const_ready = sem("u_done"), sem("u_ready"), sem("e_const_ready")
        w0_loaded = sem("w0_loaded")
        w_hi_ready, w_ready = sem("w_hi_ready"), sem("w_ready")

        def h_bank(g):
            return pair[g // 2][:, g % 2, :]

        def count(g, k):
            return SLOTS * k + g + 1

        def nodes(tile):
            return tile[:, :].rearrange("p (t f) -> p t f", t=2)

        def diag(tile):
            return tile[:, :].rearrange("p (j c) -> p j c", c=P)[:, 0:4:3, :]

        def mixed(tile):
            return tile[:, :].rearrange("p (t f) -> p t f", t=2)

        u_stage = P1[3][:, 0:4].rearrange("p (t c) -> p t c", t=2)
        staged = [(W1, slice(0, F), nodes(P0[1])), (W2, slice(0, F), nodes(P0[2])),
                  (WA, slice(0, F), nodes(P0[3])), (WB, slice(0, F), nodes(P1[1])), (WB, slice(F, 2 * F), nodes(P1[2])),
                  (WA, slice(F, FA), u_stage)]
        bk_in = sb("bk_in", [P, 3 * F])
        c_loads = [(P1[0], wvT), (aw_sb, aw), (bv_sb, bv), (P0[1], w1), (P0[2], w2), (P0[3], wk[0]), (P1[1], wk[1]),
                   (P1[2], wk[2])]
        C_LOADED = 16 * (len(c_loads) + 4)

        block = ctx.enter_context(nc.Block())

        @block.sync
        def _(sp):
            def graph(dram, g, k):
                return dram[bass.ds(k * SLOTS + g, 1)].rearrange("a p c -> (a p) c")

            def load_xT(g, kn, before=True):
                if before:
                    sp.wait_ge(s1_done, count(g, kn - 1))
                sp.dma_start(xT_in[g][:, :], graph(xT, g, kn)).then_inc(xT_loaded[g], 16)

            def load_x(g, kn, before=True):
                if before:
                    sp.wait_ge(absum_ready[g], kn)
                sp.dma_start(X0[g][:, :], graph(x, g, kn)).then_inc(x_loaded[g], 16)

            def load_adj(g, kn, before=True):
                if before:
                    sp.wait_ge(diag_ready[g], kn)
                sp.dma_start(adj_in[g][:, :], graph(adjT, g, kn)).then_inc(adj_loaded[g], 16)

            def load_adj3(g, k, before=True):
                if before:
                    sp.wait_ge(al_ready[g], k)
                sp.dma_start(adj3_in[g][:, :], graph(adjT, g, k)).then_inc(adj3_loaded[g], 16)

            def store(g, k):
                sp.wait_ge(x_ready[3][g], k + 1)
                sp.dma_start(graph(out, g, k), X3[g][:, :]).then_inc(x3_free[g], 16)

            def iteration(k, left):
                if left >= 2:
                    for g in range(SLOTS):
                        load_xT(g, k + 2)
                if left >= 1:
                    for g in range(SLOTS):
                        load_adj3(g, k + 1)
                if left >= 2:
                    for load in (load_x, load_adj):
                        for g in range(SLOTS):
                            load(g, k + 2)
                for g in range(SLOTS):
                    store(g, k)

            for load in (load_xT, load_adj, load_x, load_adj3):
                for g in range(SLOTS):
                    load(g, 0, before=False)
            for load in (load_xT, load_x, load_adj):
                for g in range(SLOTS):
                    load(g, 1)
            with sp.Fori(0, GROUPS - 2) as k:
                iteration(k, 2)
            iteration(GROUPS - 2, 1)
            iteration(GROUPS - 1, 0)
            for g in range(SLOTS):
                sp.wait_ge(x3_free[g], 16 * GROUPS + 16)

        @block.tensor
        def _(pe):
            mm = nc.tensor.matmul

            def product(dst, lhs, rhs):
                for i, o in enumerate(dst):
                    for t in range(2):
                        mm(o, lhs(1, t, i), rhs(0, t), start=t == 0, stop=False)
                        mm(o, lhs(0, t, i), rhs(1, t), start=False, stop=False)
                        last = mm(o, lhs(0, t, i), rhs(0, t), start=False, stop=t == 1)
                return last

            def product_whole(dst, lhs, rhs):
                for i, o in enumerate(dst):
                    for t in range(2):
                        last = mm(o, lhs[:, t, i * P:(i + 1) * P], rhs[:, t, :], start=t == 0, stop=t == 1)
                return last

            def cols(parts, g):
                return lambda s, t, i: parts[s][g][:, t * N + i * P:t * N + (i + 1) * P]

            def rows(parts, g):
                return lambda s, t: parts[s][g][:, t * N:(t + 1) * N]

            adj, nod, fea = (adj_hi, adj_lo), (nod_hi, nod_lo), (fea_hi, fea_lo)

            def halves(g):
                return [ring[g][:, 0:N], ring[g][:, N:2 * N]]

            def s1(g, kn, first):
                pe.wait_ge(xT_loaded[g], 16 * kn + 16)
                if not first:
                    pe.wait_ge(Q_ready, count(2 + g // 2, kn - 2))
                elif kn == 1:
                    pe.wait_ge(z0_ready, count(2 + g // 2, 0))
                product_whole([h_bank(g)[:, 0:N], h_bank(g)[:, N:2 * N]], nodes(xT_in[g]), W0).then_inc(s1_done, 1)

            def s2(g, kn):
                pe.wait_ge(h_ready, count(min(2 * g + 1, 3), kn))
                pe.wait_ge(adj_ready, count(g, kn))
                if g >= 2:
                    pe.wait_ge(z0_ready, count(g - 2, kn))
                product([pair[g % 2][:, i, 0:FA] for i in range(2)], cols(adj, g),
                        lambda s, t: mixed((h_hi, h_lo)[s][g])[:, t, :]).then_inc(s2_done, 1)

            def s3(g, kn, first):
                pe.wait_ge(x1_lo_ready, count(g, kn))
                if not first:
                    pe.wait_ge(e_ready, count(g, kn - 1))
                product(halves(g), cols(nod, g), rows(adj, g)).then_inc(s3_done[g], 1)

            def s4(g, kn):
                pe.wait_ge(t1_ready, count(g, kn))
                product(halves(g), cols(fea, g), lambda s, t: W1[s][:, t, :]).then_inc(s4_done, 1)

            def s5(g, kn, first):
                pe.wait_ge(xd_lo_ready, count(g, kn))
                pe.wait_ge(diag_ready[g], kn + 1)
                if not first:
                    pe.wait_ge(z3_ready, count(g, kn - 1))
                product(halves(g), cols(nod, g), rows(adj, g)).then_inc(s5_done[g], 1)

            def s6(g, k):
                pe.wait_ge(t2_ready, count(g, k))
                product(halves(g), cols(fea, g), lambda s, t: W2[s][:, t, :]).then_inc(s6_done, 1)

            def s7(g, k):
                pe.wait_ge(x_ready[2][g], k + 1)
                for f in range(2):
                    for t in range(2):
                        last = nc.tensor.transpose(ring[g][:, f * N + t * P:f * N + (t + 1) * P],
                                                   nodes(X3[g])[:, t, f * P:(f + 1) * P], ident[:, :])
                last.then_inc(s7_done[g], 1)

            def s8a(g, k, last):
                pe.wait_ge(x3T_ready, count(g, k))
                if g >= 1:
                    pe.wait_ge(P0_ready, count(g - 1, k))
                elif not last:
                    pe.wait_ge(z0_ready, count(2, k + 1))
                product([pair[0][:, i, 0:FA] for i in range(2)], cols(fea, g),
                        lambda s, t: WA[s][:, t, :]).then_inc(s8a_done, 1)

            def s8b(g, k, last):
                if g >= 1:
                    pe.wait_ge(P12_ready, count(g - 1, k))
                elif not last:
                    pe.wait_ge(z0_ready, count(3, k + 1))
                product([pair[1][:, i, :] for i in range(2)], cols(fea, g),
                        lambda s, t: WB[s][:, t, :]).then_inc(s8b_done, 1)

            def s9(g, k):
                pe.wait_ge(logit_ready, count(g, k))
                for t in range(2):
                    last = nc.tensor.transpose(ring[g][:, t * P:(t + 1) * P],
                                               logit[g][:, 4 + t:5 + t].to_broadcast([P, P]), ident[:, :])
                last.then_inc(s9_done, 1)

            def s10(g, k):
                pe.wait_ge(al_ready[g], k + 1)
                pe.wait_ge(P12_ready, count(SLOTS - 1, k))
                if g == 0:
                    pe.wait_ge(P0_ready, count(SLOTS - 1, k))
                if g >= 2:
                    pe.wait_ge(Q_ready, count(g - 2, k))
                product_whole([pair[g % 2][:, i, 0:FA] for i in range(2)], nodes(tmp[g]), mixed(P2[g])).then_inc(s10_done, 1)

            def s11(g, k, last):
                pe.wait_ge(Q_ready, count(g, k))
                if not last:
                    pe.wait_ge(y_ready[1][g], k + 2)
                product_whole(halves(g), nodes(tmp[g]), nodes(P1[g])).then_inc(s11_done, 1)

            def iteration(k, left, first=False):
                if not first:
                    for g in (0, 1, 2):
                        s6(g, k)
                if left >= 1:
                    for g in (0, 1):
                        s2(g, k + 1)
                if not first:
                    s6(3, k)
                if left >= 1:
                    s2(2, k + 1)
                if not first:
                    s7(0, k)
                if left >= 1:
                    s2(3, k + 1)
                if not first:
                    s8a(0, k, left == 0)
                    s7(1, k)
                    s8b(0, k, left == 0)
                    s7(2, k)
                    s9(0, k)
                    s8a(1, k, left == 0)
                    s8b(1, k, left == 0)
                    s8a(2, k, left == 0)
                    s7(3, k)
                    s9(1, k)
                    s8b(2, k, left == 0)
                    s9(2, k)
                    s8a(3, k, left == 0)
                if left >= 1:
                    for g in (0, 1):
                        s3(g, k + 1, first)
                if not first:
                    s8b(3, k, left == 0)
                    s9(3, k)
                if left >= 1:
                    for g in (0, 1):
                        s4(g, k + 1)
                    s3(2, k + 1, first)
                if not first:
                    for g in (0, 1):
                        s10(g, k)
                if left >= 1:
                    s4(2, k + 1)
                    s3(3, k + 1, first)
                if not first:
                    for g in (0, 1):
                        s11(g, k, left == 0)
                if left >= 1:
                    s5(0, k + 1, first)
                    s4(3, k + 1)
                if not first:
                    for g in (2, 3):
                        s10(g, k)
                    for g in (2, 3):
                        s11(g, k, left == 0)
                if left >= 2:
                    for g in (0, 1, 2):
                        s1(g, k + 2, first)
                if left >= 1:
                    for g in (1, 2, 3):
                        s5(g, k + 1, first)
                if left >= 2:
                    s1(3, k + 2, first)

            pe.wait_ge(w0_loaded, 16)
            for g in range(SLOTS):
                s1(g, 0, True)
            pe.wait_ge(c_loaded, C_LOADED)
            for f in range(2):
                for t in range(2):
                    mm(ring[0][:, 2 * f:2 * f + 2], P1[0][:, t * F + f * P:t * F + (f + 1) * P], aw_sb[:, t, :],
                       start=t == 0, stop=t == 1)
            for t in range(2):
                last = mm(ring[0][:, 4:6], bv_sb[:, t:t + 1].to_broadcast([P, P]), aw_sb[:, t, :], start=t == 0, stop=t == 1)
            last.then_inc(u_done, 1)
            pe.wait_ge(w_ready, 1)
            iteration(-1, 2, first=True)
            with pe.Fori(0, GROUPS - 2) as k:
                iteration(k, 2)
            iteration(GROUPS - 2, 1)
            iteration(GROUPS - 1, 0)

        @block.scalar
        def _(act):
            def copy(dst, src):
                return nc.scalar.activation(dst, src, ACT.Copy)

            def h_hi_part(g, kn):
                act.wait_ge(s1_done, count(g, kn))
                copy(mixed(h_hi[g])[:, :, 0:F], nodes(h_bank(g))).then_inc(h_hi_ready, 1)

            def z0(g, kn):
                act.wait_ge(rinv0_ready, count(g, kn))
                for t in range(2):
                    last = nc.scalar.activation(nodes(X1[g])[:, t, :], pair[g % 2][:, t, 0:F], ACT.Identity,
                                                scale=rinv[g][:, t:t + 1])
                last.then_inc(z0_ready, 1)

            def x1_hi(g, kn):
                act.wait_ge(x_ready[0][g], kn + 1)
                copy(nod_hi[g][:, :], X1[g][:, :]).then_inc(x1_hi_ready, 1)

            def x1_sum(g, kn):
                act.wait_ge(x_ready[0][g], kn + 1)
                for t in range(2):
                    last = nc.scalar.activation(X0[g][:, t * F:(t + 1) * F], nodes(X1[g])[:, t, :], ACT.Abs,
                                                accum_out=absum[g][:, t:t + 1])
                last.then_inc(absum_ready[g], 1)

            def adj_hi_part(g, kn, first):
                act.wait_ge(adj_loaded[g], 16 * kn + 16)
                if not first:
                    act.wait_ge(s5_done[g], kn)
                copy(adj_hi[g][:, :], adj_in[g][:, :]).then_inc(adj_hi_ready, 1)

            def from_ring(g, done, k, dst, ready):
                act.wait_ge(done[g], k + 1)
                copy(dst[g][:, :], ring[g][:, :]).then_inc(ready, 1)

            def xd_hi(g, k):
                act.wait_ge(x_ready[1][g], k + 1)
                for t in range(2):
                    last = nc.scalar.activation(nod_hi[g][:, t * F:(t + 1) * F], nodes(X2[g])[:, t, :], ACT.Identity,
                                                scale=rstd[0][g][:, 2 + t:3 + t])
                last.then_inc(xd_hi_ready, 1)

            def diag_hi(g, k):
                act.wait_ge(dsum_ready, count(g, k))
                act.wait_ge(s3_done[g], k + 1)
                copy(diag(adj_hi[g]), diag(adj_in[g])).then_inc(dhi_ready, 1)

            def p12(g, k):
                act.wait_ge(s8b_done, count(g, k))
                copy(nodes(P1[g]), pair[1][:, :, 0:F])
                copy(mixed(P2[g])[:, :, 0:F], pair[1][:, :, F:2 * F]).then_inc(P12_ready, 1)

            def slope(g, k):
                act.wait_ge(s9_done, count(g, k))
                act.wait_ge(logit_ready, count(g, k))
                for t in range(2):
                    last = nc.scalar.activation(tmp[g][:, t * N:(t + 1) * N], ring[g][:, 0:N], ACT.Identity,
                                                scale=0.2, bias=logit[g][:, 2 + t:3 + t])
                last.then_inc(sl_ready, 1)

            def exp(g, k):
                act.wait_ge(e_ready, count(g, k))
                nc.scalar.activation(tmp[g][:, :], tmp[g][:, :], ACT.Exp).then_inc(ex_ready, 1)

            def norm(l, g, k):
                act.wait_ge(nmr_ready[l], count(g, k))
                if l == 2:
                    act.wait_ge(x3_free[g], 16 * k + 16)
                for t in range(2):
                    last = nc.scalar.activation(nodes(X3[g])[:, t, :], nodes(X[l][g])[:, t, :], ACT.Identity,
                                                scale=rstd[l][g][:, t:t + 1], bias=nmr[l][g][:, t:t + 1])
                last.then_inc(x_ready[l][g], 1)

            def iteration(k, left, first=False):
                if left >= 1:
                    h_hi_part(0, k + 1)
                    adj_hi_part(0, k + 1, first)
                    h_hi_part(1, k + 1)
                    adj_hi_part(1, k + 1, first)
                    for g in (2, 3):
                        h_hi_part(g, k + 1)
                    for g in (2, 3):
                        adj_hi_part(g, k + 1, first)
                    z0(0, k + 1)
                if not first:
                    norm(2, 0, k)
                if left >= 1:
                    z0(1, k + 1)
                if not first:
                    from_ring(0, s7_done, k, fea_hi, x3T_hi_ready)
                if left >= 1:
                    z0(2, k + 1)
                if not first:
                    norm(2, 1, k)
                if left >= 1:
                    z0(3, k + 1)
                if not first:
                    from_ring(1, s7_done, k, fea_hi, x3T_hi_ready)
                    norm(2, 2, k)
                    p12(0, k)
                    slope(0, k)
                    from_ring(2, s7_done, k, fea_hi, x3T_hi_ready)
                    norm(2, 3, k)
                    p12(1, k)
                    from_ring(3, s7_done, k, fea_hi, x3T_hi_ready)
                    slope(1, k)
                if left >= 1:
                    for g in (0, 1):
                        x1_hi(g, k + 1)
                if not first:
                    for g in (0, 1):
                        exp(g, k)
                    p12(2, k)
                    slope(2, k)
                if left >= 1:
                    for g in (0, 1):
                        x1_sum(g, k + 1)
                    for g in (0, 1):
                        from_ring(g, s3_done, k + 1, fea_hi, t1_hi_ready)
                    x1_hi(2, k + 1)
                if not first:
                    p12(3, k)
                if left >= 1:
                    x1_sum(2, k + 1)
                if not first:
                    exp(2, k)
                if left >= 1:
                    from_ring(2, s3_done, k + 1, fea_hi, t1_hi_ready)
                if not first:
                    slope(3, k)
                if left >= 1:
                    x1_hi(3, k + 1)
                    x1_sum(3, k + 1)
                if not first:
                    exp(3, k)
                if left >= 1:
                    xd_hi(0, k + 1)
                    diag_hi(0, k + 1)
                    from_ring(3, s3_done, k + 1, fea_hi, t1_hi_ready)
                    from_ring(0, s5_done, k + 1, fea_hi, t2_hi_ready)
                    for g in (1, 2, 3):
                        diag_hi(g, k + 1)
                if not first:
                    norm(3, 0, k)
                if left >= 1:
                    for g in (1, 2, 3):
                        xd_hi(g, k + 1)
                if not first:
                    norm(3, 1, k)
                if left >= 1:
                    for g in (1, 2):
                        from_ring(g, s5_done, k + 1, fea_hi, t2_hi_ready)
                if not first:
                    norm(3, 2, k)
                if left >= 1:
                    from_ring(3, s5_done, k + 1, fea_hi, t2_hi_ready)
                if not first:
                    norm(3, 3, k)

            act.dma_start(W0[:, :, :], w0.rearrange("p (t f) -> p t f", t=2)).then_inc(w0_loaded, 16)
            for tile, dram in c_loads:
                act.dma_start(tile[:, :], dram).then_inc(c_loaded, 16)
            act.dma_start(b0_bc[:, :], b0.to_broadcast([P, F])).then_inc(c_loaded, 16)
            act.dma_start(b2_bc[:, :], b2.to_broadcast([P, F])).then_inc(c_loaded, 16)
            act.dma_start(bk_in[:, :], bk.to_broadcast([P, 3 * F])).then_inc(c_loaded, 16)
            act.dma_start(ab_bc[:, :], ab.to_broadcast([P, 1])).then_inc(c_loaded, 16)
            act.wait_ge(c_loaded, C_LOADED)
            act.wait_ge(u_ready, 1)
            for w, columns, stage in staged:
                last = copy(w[0][:, :, columns], stage)
            last.then_inc(w_hi_ready, 1)
            iteration(-1, 2, first=True)
            with act.Fori(0, GROUPS - 2) as k:
                iteration(k, 2)
            iteration(GROUPS - 2, 1)
            iteration(GROUPS - 1, 0)

        @block.gpsimd
        def _(pool):
            ts, tt = nc.gpsimd.tensor_scalar, nc.gpsimd.tensor_tensor

            def x_bias(g, kn):
                pool.wait_ge(x_loaded[g], 16 * kn + 16)
                tt(nodes(X0[g]), nodes(X0[g]), b0_bc[:, :].unsqueeze(1).to_broadcast([P, 2, F]), ALU.add).then_inc(xb_ready, 1)

            def adj_lo_part(g, kn):
                pool.wait_ge(adj_hi_ready, count(g, kn))
                tt(adj_lo[g][:, :], adj_in[g][:, :], adj_hi[g][:, :], ALU.subtract).then_inc(adj_ready, 1)

            def x1_lo(g, kn):
                pool.wait_ge(x1_hi_ready, count(g, kn))
                tt(nod_lo[g][:, :], X1[g][:, :], nod_hi[g][:, :], ALU.subtract).then_inc(x1_lo_ready, 1)

            def y0(g, kn):
                pool.wait_ge(xb_ready, count(g, kn))
                pool.wait_ge(z0_ready, count(g, kn))
                tt(X0[g][:, :], X0[g][:, :], X1[g][:, :], ALU.add).then_inc(y_ready[0][g], 1)

            def scales(l, g, k):
                n = 4 if l == 0 else 2
                pool.wait_ge(mv_ready[l], count(g, k))
                tt(powin[l][g][:, 0:2], mv[l][g][:, 1:4:2], eps[:, :], ALU.add).then_inc(pin_ready[l], 1)
                pool.wait_ge(pin_ready[l], count(g, k))
                if l == 0:
                    pool.wait_ge(deg_ready, count(g, k))
                tt(rstd[l][g][:, 0:n], powin[l][g][:, 0:n], minus_half[:, 0:n], ALU.pow).then_inc(rstd_ready[l], 1)
                if l == 1:
                    pool.wait_ge(rstd_ready[l], count(g, k))
                    pool.wait_ge(mask_ready, count(g, k))
                    tt(rstd[l][g][:, 0:2], rstd[l][g][:, 0:2], mask[g][:, :], ALU.mult).then_inc(rstdm_ready, 1)
                if l >= 2:
                    pool.wait_ge(rstd_ready[l], count(g, k))
                    pool.wait_ge(nm_ready[l], count(g, k))
                    tt(nmr[l][g][:, :], nmean[l][g][:, :], rstd[l][g][:, 0:2], ALU.mult).then_inc(nmr_ready[l], 1)

            def norm0(g, k):
                pool.wait_ge(pool_c, 3)
                pool.wait_ge(rstd_ready[0], count(g, k))
                pool.wait_ge(nm_ready[0], count(g, k))
                for t in range(2):
                    last = ts(nodes(X1[g])[:, t, :], nodes(X0[g])[:, t, :], nmean[0][g][:, t:t + 1], rstd[0][g][:, t:t + 1],
                              ALU.add, ALU.mult)
                last.then_inc(x_ready[0][g], 1)

            def alpha(g, k):
                pool.wait_ge(ex_ready, count(g, k))
                pool.wait_ge(adj3_loaded[g], 16 * k + 16)
                tt(tmp[g][:, :], tmp[g][:, :], adj3_in[g][:, :], ALU.mult).then_inc(al_ready[g], 1)

            def diag_sum(g, k):
                pool.wait_ge(adj_ready, count(g, k))
                ident2 = ident[:, :].unsqueeze(1).to_broadcast([P, 2, P])
                tt(diag(adj_in[g]), diag(adj_in[g]), ident2, ALU.add).then_inc(dsum_ready, 1)

            def diag_lo(g, k):
                pool.wait_ge(dhi_ready, count(g, k))
                tt(diag(adj_lo[g]), diag(adj_in[g]), diag(adj_hi[g]), ALU.subtract).then_inc(diag_ready[g], 1)

            def iteration(k, left, first=False):
                if left >= 1:
                    for g in range(SLOTS):
                        adj_lo_part(g, k + 1)
                if not first:
                    scales(2, 0, k)
                if left >= 1:
                    y0(0, k + 1)
                if not first:
                    for g in (1, 2):
                        scales(2, g, k)
                if left >= 1:
                    for g in (1, 2, 3):
                        y0(g, k + 1)
                if not first:
                    scales(2, 3, k)
                if left >= 1:
                    for g in (0, 1):
                        scales(0, g, k + 1)
                    for g in (0, 1):
                        norm0(g, k + 1)
                    for g in (0, 1):
                        x1_lo(g, k + 1)
                    scales(0, 2, k + 1)
                    norm0(2, k + 1)
                if not first:
                    alpha(0, k)
                if left >= 1:
                    scales(0, 3, k + 1)
                if not first:
                    alpha(1, k)
                if left >= 1:
                    x1_lo(2, k + 1)
                    norm0(3, k + 1)
                    scales(1, 0, k + 1)
                    diag_sum(0, k + 1)
                    x1_lo(3, k + 1)
                    diag_lo(0, k + 1)
                    scales(1, 1, k + 1)
                if not first:
                    for g in (2, 3):
                        alpha(g, k)
                if left >= 2:
                    x_bias(0, k + 2)
                if left >= 1:
                    diag_sum(1, k + 1)
                if not first:
                    scales(3, 0, k)
                if left >= 1:
                    scales(1, 2, k + 1)
                    for g in (2, 3):
                        diag_sum(g, k + 1)
                    diag_lo(1, k + 1)
                    scales(1, 3, k + 1)
                if left >= 2:
                    x_bias(1, k + 2)
                if left >= 1:
                    for g in (2, 3):
                        diag_lo(g, k + 1)
                if not first:
                    scales(3, 1, k)
                if left >= 2:
                    for g in (2, 3):
                        x_bias(g, k + 2)
                if not first:
                    for g in (2, 3):
                        scales(3, g, k)

            pool.memset(ident[:, :], 0.0).then_inc(pool_c, 1)
            pool.wait_ge(pool_c, 1)
            pool.affine_select(out=ident[:, :], in_=ident[:, :], compare_op=ALU.not_equal, fill=1.0, base=0,
                               pattern=[[-1, P]], channel_multiplier=1).then_inc(pool_c, 1)
            pool.memset(minus_half[:, :], -0.5)
            pool.memset(eps[:, :], EPS).then_inc(pool_c, 1)
            pool.wait_ge(pool_c, 3)
            pool.wait_ge(c_loaded, C_LOADED)
            tt(bk_bc[:, :], bk_in[:, 0:F], bk_in[:, F:2 * F], ALU.add).then_inc(pool_c, 1)
            pool.wait_ge(pool_c, 4)
            tt(bk_bc[:, :], bk_bc[:, :], bk_in[:, 2 * F:3 * F], ALU.add).then_inc(bk_ready, 1)
            for g in range(SLOTS):
                x_bias(g, 0)
            iteration(-1, 2, first=True)
            with pool.Fori(0, GROUPS - 2) as k:
                iteration(k, 2)
            iteration(GROUPS - 2, 1)
            iteration(GROUPS - 1, 0)

        @block.vector
        def _(dve):
            ts, tt, stt = nc.vector.tensor_scalar, nc.vector.tensor_tensor, nc.vector.scalar_tensor_tensor

            def from_ring(g, hi_ready, k, ready):
                dve.wait_ge(hi_ready, count(g, k))
                tt(fea_lo[g][:, :], ring[g][:, :], fea_hi[g][:, :], ALU.subtract).then_inc(ready, 1)

            def h_lo_part(g, kn):
                dve.wait_ge(h_hi_ready, count(g, kn))
                tt(mixed(h_lo[g])[:, :, 0:F], nodes(h_bank(g)), mixed(h_hi[g])[:, :, 0:F], ALU.subtract).then_inc(h_ready, 1)

            def statistics(l, g, k):
                dve.wait_ge(y_ready[l][g], k + 1)
                for t in range(2):
                    last = nc.vector.bn_stats(stats[l][g][:, 6 * t:6 * t + 6], nodes(X[l][g])[:, t, :])
                last.then_inc(st_ready[l], 1)

            def moments(l, g, k):
                dve.wait_ge(e_const_ready, 2)
                dve.wait_ge(st_ready[l], count(g, k))
                for t in range(2):
                    last = nc.vector.bn_aggr(mv[l][g][:, 2 * t:2 * t + 2], stats[l][g][:, 6 * t:6 * t + 6])
                last.then_inc(mv_ready[l], 1)
                dve.wait_ge(mv_ready[l], count(g, k))
                ts(nmean[l][g][:, :], mv[l][g][:, 0:4:2], -1.0, None, ALU.mult).then_inc(nm_ready[l], 1)

            def sums0(g, kn):
                dve.wait_ge(s2_done, count(g, kn))
                sums = pair[g % 2][:, :, F]
                ts(powin[0][g][:, 2:4], sums, 1.0, None, ALU.add).then_inc(deg_ready, 1)
                nc.vector.reciprocal(rinv[g][:, :], sums).then_inc(rinv0_ready, 1)

            def norm(l, g, k):
                dve.wait_ge(rstdm_ready, count(g, k))
                dve.wait_ge(nm_ready[l], count(g, k))
                for t in range(2):
                    last = ts(nodes(X[l + 1][g])[:, t, :], nodes(X[l][g])[:, t, :], nmean[l][g][:, t:t + 1], rstd[l][g][:, t:t + 1],
                              ALU.add, ALU.mult)
                last.then_inc(x_ready[l][g], 1)

            def mask_of_x1(g, kn):
                dve.wait_ge(absum_ready[g], kn + 1)
                ts(mask[g][:, :], absum[g][:, :], 0.0, None, ALU.is_gt).then_inc(mask_ready, 1)

            def y1(g, k):
                dve.wait_ge(s4_done, count(g, k))
                dve.wait_ge(absum_ready[g], k + 1)
                stt(X1[g][:, :], ring[g][:, :], 0.0, X1[g][:, :], ALU.max, ALU.add).then_inc(y_ready[1][g], 1)

            def xd_lo(g, k):
                dve.wait_ge(xd_hi_ready, count(g, k))
                for t in range(2):
                    last = stt(nod_lo[g][:, t * F:(t + 1) * F], nodes(X2[g])[:, t, :], rstd[0][g][:, 2 + t:3 + t],
                               nod_hi[g][:, t * F:(t + 1) * F], ALU.mult, ALU.subtract)
                last.then_inc(xd_lo_ready, 1)

            def y2(g, k):
                dve.wait_ge(s6_done, count(g, k))
                for t in range(2):
                    last = stt(tmp[g][:, t * F:(t + 1) * F], ring[g][:, t * N:(t + 1) * N], rstd[0][g][:, 2 + t:3 + t], b2_bc[:, :],
                               ALU.mult, ALU.add)
                last.then_inc(z2_ready, 1)

            def y2b(g, k):
                dve.wait_ge(z2_ready, count(g, k))
                stt(X2[g][:, :], tmp[g][:, :], 0.0, X2[g][:, :], ALU.max, ALU.add).then_inc(y_ready[2][g], 1)

            def logit_of(g, k):
                dve.wait_ge(s8a_done, count(g, k))
                ts(logit[g][:, 0:2], pair[0][:, :, F], e_const[:, 0:1], None, ALU.add)
                ts(logit[g][:, 2:4], pair[0][:, :, F], e_const[:, 0:1], 0.2, ALU.add, ALU.mult)
                nc.vector.tensor_copy(logit[g][:, 4:6], pair[0][:, :, F + 1]).then_inc(logit_ready, 1)

            def p0(g, k):
                dve.wait_ge(s8a_done, count(g, k))
                tt(nodes(P0[g]), pair[0][:, :, 0:F], bk_bc[:, :].unsqueeze(1).to_broadcast([P, 2, F]), ALU.add).then_inc(P0_ready, 1)

            def leaky(g, k):
                dve.wait_ge(sl_ready, count(g, k))
                for t in range(2):
                    last = stt(tmp[g][:, t * N:(t + 1) * N], ring[g][:, 0:N], logit[g][:, t:t + 1], tmp[g][:, t * N:(t + 1) * N],
                               ALU.add, ALU.max)
                last.then_inc(e_ready, 1)

            def q(g, k):
                dve.wait_ge(s10_done, count(g, k))
                ts(rinv[g][:, :], pair[g % 2][:, :, F], 1e-12, None, ALU.add).then_inc(asum_ready, 1)
                dve.wait_ge(asum_ready, count(g, k))
                nc.vector.reciprocal(rinv[g][:, :], rinv[g][:, :]).then_inc(rinv3_ready, 1)
                dve.wait_ge(rinv3_ready, count(g, k))
                for t in range(2):
                    last = stt(nodes(P1[g])[:, t, :], pair[g % 2][:, t, 0:F], rinv[g][:, t:t + 1], nodes(P1[g])[:, t, :],
                               ALU.mult, ALU.add)
                last.then_inc(Q_ready, 1)

            def z3(g, k):
                dve.wait_ge(s11_done, count(g, k))
                for t in range(2):
                    last = stt(nodes(P0[g])[:, t, :], ring[g][:, t * F:(t + 1) * F], rinv[g][:, t:t + 1], nodes(P0[g])[:, t, :],
                               ALU.mult, ALU.add)
                last.then_inc(z3_ready, 1)

            def y3(g, k):
                dve.wait_ge(z3_ready, count(g, k))
                stt(X3[g][:, :], P0[g][:, :], 0.0, X3[g][:, :], ALU.max, ALU.add).then_inc(y_ready[3][g], 1)

            def iteration(k, left, first=False):
                if left >= 1:
                    h_lo_part(0, k + 1)
                if not first:
                    y2(0, k)
                if left >= 1:
                    for g in (1, 2, 3):
                        h_lo_part(g, k + 1)
                if not first:
                    y2b(0, k)
                    statistics(2, 0, k)
                if left >= 1:
                    sums0(0, k + 1)
                if not first:
                    moments(2, 0, k)
                    y2(1, k)
                    y2b(1, k)
                if left >= 1:
                    sums0(1, k + 1)
                if not first:
                    statistics(2, 1, k)
                    y2(2, k)
                    moments(2, 1, k)
                if left >= 1:
                    sums0(2, k + 1)
                if not first:
                    y2b(2, k)
                    from_ring(0, x3T_hi_ready, k, x3T_ready)
                    statistics(2, 2, k)
                if left >= 1:
                    sums0(3, k + 1)
                if not first:
                    moments(2, 2, k)
                    y2(3, k)
                    logit_of(0, k)
                    y2b(3, k)
                    p0(0, k)
                if left >= 1:
                    statistics(0, 0, k + 1)
                if not first:
                    from_ring(1, x3T_hi_ready, k, x3T_ready)
                    statistics(2, 3, k)
                if left >= 1:
                    moments(0, 0, k + 1)
                if not first:
                    moments(2, 3, k)
                    logit_of(1, k)
                    p0(1, k)
                    from_ring(2, x3T_hi_ready, k, x3T_ready)
                if left >= 1:
                    statistics(0, 1, k + 1)
                    moments(0, 1, k + 1)
                if not first:
                    leaky(0, k)
                if left >= 1:
                    for g in (2, 3):
                        statistics(0, g, k + 1)
                if not first:
                    logit_of(2, k)
                    p0(2, k)
                    from_ring(3, x3T_hi_ready, k, x3T_ready)
                    leaky(1, k)
                if left >= 1:
                    for g in (2, 3):
                        moments(0, g, k + 1)
                if not first:
                    leaky(2, k)
                    logit_of(3, k)
                if left >= 1:
                    mask_of_x1(0, k + 1)
                    from_ring(0, t1_hi_ready, k + 1, t1_ready)
                if not first:
                    p0(3, k)
                if left >= 1:
                    from_ring(1, t1_hi_ready, k + 1, t1_ready)
                    y1(0, k + 1)
                    statistics(1, 0, k + 1)
                    y1(1, k + 1)
                    mask_of_x1(1, k + 1)
                    moments(1, 0, k + 1)
                    mask_of_x1(2, k + 1)
                    statistics(1, 1, k + 1)
                    from_ring(2, t1_hi_ready, k + 1, t1_ready)
                    norm(1, 0, k + 1)
                if not first:
                    leaky(3, k)
                    for g in (0, 1):
                        q(g, k)
                if left >= 1:
                    moments(1, 1, k + 1)
                    xd_lo(0, k + 1)
                    y1(2, k + 1)
                    from_ring(3, t1_hi_ready, k + 1, t1_ready)
                    statistics(1, 2, k + 1)
                    mask_of_x1(3, k + 1)
                if not first:
                    z3(0, k)
                    y3(0, k)
                    z3(1, k)
                if left >= 1:
                    moments(1, 2, k + 1)
                if not first:
                    statistics(3, 0, k)
                    y3(1, k)
                if left >= 1:
                    y1(3, k + 1)
                if not first:
                    moments(3, 0, k)
                if left >= 1:
                    statistics(1, 3, k + 1)
                if not first:
                    q(2, k)
                if left >= 1:
                    norm(1, 1, k + 1)
                if not first:
                    q(3, k)
                if left >= 1:
                    moments(1, 3, k + 1)
                if not first:
                    statistics(3, 1, k)
                    z3(2, k)
                    moments(3, 1, k)
                    y3(2, k)
                    z3(3, k)
                if left >= 1:
                    norm(1, 2, k + 1)
                    xd_lo(1, k + 1)
                    norm(1, 3, k + 1)
                    xd_lo(2, k + 1)
                if not first:
                    statistics(3, 2, k)
                    y3(3, k)
                    moments(3, 2, k)
                if left >= 1:
                    xd_lo(3, k + 1)
                if not first:
                    statistics(3, 3, k)
                if left >= 1:
                    from_ring(0, t2_hi_ready, k + 1, t2_ready)
                if not first:
                    moments(3, 3, k)
                if left >= 1:
                    for g in (1, 2, 3):
                        from_ring(g, t2_hi_ready, k + 1, t2_ready)

            for g in range(SLOTS):
                nc.vector.memset(mixed(h_hi[g])[:, :, F:FA].bitcast(FP), 1.0)
                nc.vector.memset(mixed(P2[g])[:, :, F:FA], 1.0)
                nc.vector.memset(mixed(h_lo[g])[:, :, F:FA].bitcast(FP), 0.0).then_inc(x3_free[g], 16)
            dve.wait_ge(u_done, 1)
            dve.wait_ge(c_loaded, C_LOADED)
            nc.vector.tensor_copy(u_stage, ring[0][:, 0:4].rearrange("p (t c) -> p t c", t=2)).then_inc(u_ready, 1)
            ts(e_const[:, :], ring[0][:, 4:5], ab_bc[:, 0:1], None, ALU.add).then_inc(e_const_ready, 1)
            dve.wait_ge(e_const_ready, 1)
            tt(e_const[:, :], ring[0][:, 5:6], e_const[:, :], ALU.add).then_inc(e_const_ready, 1)
            dve.wait_ge(e_const_ready, 2)
            dve.wait_ge(bk_ready, 1)
            dve.wait_ge(w_hi_ready, 1)
            for w, columns, stage in staged:
                last = tt(w[1][:, :, columns], stage, w[0][:, :, columns], ALU.subtract)
            last.then_inc(w_ready, 1)
            iteration(-1, 2, first=True)
            with dve.Fori(0, GROUPS - 2) as k:
                iteration(k, 2)
            iteration(GROUPS - 2, 1)
            iteration(GROUPS - 1, 0)


def kernel(x, adj, L0_gnn_W, L0_gnn_b, L1_gnn_kernel, L2_gnn_kernel, L2_gnn_bias, L3_gnn_Wv, L3_gnn_bv, L3_gnn_aw,
           L3_gnn_ab, L3_gnn_Wk, L3_gnn_bk):
    import numpy as np
    import concourse.bacc as bacc
    from concourse.bass_utils import run_bass_kernel_spmd

    B, N, F = x.shape
    C = 2 * N

    def by_feature(w):
        w = np.asarray(w)
        return w.reshape(2, P, -1).transpose(1, 0, 2).reshape(P, -1)

    def nodes_last(a):
        return a.reshape(B, -1, P, 2).transpose(0, 1, 3, 2).reshape(B, -1, N)

    x, adj = np.asarray(x), np.asarray(adj)
    xT = nodes_last(x.transpose(0, 2, 1)).reshape(B, 2, P, N).transpose(0, 2, 1, 3).reshape(B, P, C)
    adjT = nodes_last(adj.transpose(0, 2, 1)).reshape(B, P, C)
    data = {
        "x": x.reshape(B, P, C), "xT": xT, "adjT": adjT,
        "w0": by_feature(L0_gnn_W), "w1": by_feature(L1_gnn_kernel), "w2": by_feature(L2_gnn_kernel),
        "wk": np.stack([by_feature(w) for w in np.asarray(L3_gnn_Wk)]),
        "wvT": by_feature(np.asarray(L3_gnn_Wv).T),
        "aw": by_feature(np.asarray(L3_gnn_aw).reshape(2, F).T), "bv": by_feature(np.asarray(L3_gnn_bv).reshape(F, 1)),
        "ab": np.asarray(L3_gnn_ab).reshape(1, 1), "b0": np.asarray(L0_gnn_b).reshape(1, F),
        "b2": np.asarray(L2_gnn_bias).reshape(1, F), "bk": np.asarray(L3_gnn_bk).reshape(1, 3 * F),
    }
    data = {name: np.ascontiguousarray(a) for name, a in data.items()}
    nc = bacc.Bacc("TRN2", target_bir_lowering=False, num_devices=1)
    drams = {name: nc.dram_tensor(f"{name}_dram", a.shape, mybir.dt.from_np(a.dtype), kind="ExternalInput").ap()
             for name, a in data.items()}
    out = nc.dram_tensor("out_dram", (B, P, C), FP, kind="ExternalOutput").ap()
    build(nc, out=out, **drams)
    result = run_bass_kernel_spmd(nc, [{f"{name}_dram": a for name, a in data.items()}], core_ids=[0])
    return result.results[0]["out_dram"].reshape(B, N, F)
```

```python
from contextlib import ExitStack

import concourse.bass as bass
from concourse import mybir

P = 128
SLOTS = 4
EPS = 1e-5
FP = mybir.dt.float32
FR = mybir.dt.float32r
ALU = mybir.AluOpType
ACT = mybir.ActivationFunctionType


def build(nc, x, xT, adjT, w0, w1, w2, wk, wvT, aw, bv, ab, b0, b2, bk, out):
    B = x.shape[0]
    N = x.shape[2] // 2
    F = N
    GROUPS = B // SLOTS
    C = 2 * N
    FA = F + 2

    with ExitStack() as ctx:
        def sb(name, shape, dt=FP):
            return ctx.enter_context(nc.sbuf_tensor(name, shape, dt))

        def sem(name):
            return ctx.enter_context(nc.semaphore(name))

        def sem4(name):
            return [sem(f"{name}{g}") for g in range(SLOTS)]

        def slots(name, cols, dt=FP):
            return [sb(f"{name}{g}", [P, cols], dt) for g in range(SLOTS)]

        W0 = [sb(f"W0_{s}", [P, 2, F], FR) for s in ("hi", "lo")]
        W1 = [sb(f"W1_{s}", [P, 2, F], FR) for s in ("hi", "lo")]
        W2 = [sb(f"W2_{s}", [P, 2, F], FR) for s in ("hi", "lo")]
        WA = [sb(f"WA_{s}", [P, 2, FA], FR) for s in ("hi", "lo")]
        WB = [sb(f"WB_{s}", [P, 2, 2 * F], FR) for s in ("hi", "lo")]
        b0_bc = sb("b0_bc", [P, F])
        b2_bc = sb("b2_bc", [P, F])
        bk_bc = sb("bk_bc", [P, FA])
        ident = sb("ident", [P, P])
        minus_half = sb("minus_half", [P, 4])
        ab_bc = sb("ab_bc", [P, 1])
        aw_sb = sb("aw_sb", [P, 2, 2])
        bv_sb = sb("bv_sb", [P, 2])

        xT_in = slots("xT_in", C)
        xT_hi, xT_lo = slots("xT_hi", C, FR), slots("xT_lo", C, FR)
        adj_in = slots("adj_in", C)
        adj3_in = slots("adj3_in", C)
        X0 = slots("X0_", C)
        X1 = slots("X1_", C)
        X2 = slots("X2_", C)
        X3 = slots("X3_", C)
        adj_hi, adj_lo = slots("adj_hi", C, FR), slots("adj_lo", C, FR)
        h_hi, h_lo = slots("h_hi", 2 * FA, FR), slots("h_lo", 2 * FA, FR)
        nod_hi, nod_lo = slots("nod_hi", C, FR), slots("nod_lo", C, FR)
        fea_hi, fea_lo = slots("fea_hi", C, FR), slots("fea_lo", C, FR)
        tmp = slots("tmp", C)
        P0 = slots("P0_", 2 * FA)
        P1 = slots("P1_", C)
        alpha_hi, alpha_lo = slots("alpha_hi", C, FR), slots("alpha_lo", C, FR)
        stats = [slots(f"stats{l}_", 12) for l in range(4)]
        mv = [slots(f"mv{l}_", 4) for l in range(4)]
        nmean = [slots(f"nmean{l}_", 2) for l in range(4)]
        powin = [slots(f"powin{l}_", 4) for l in range(4)]
        rstd = [slots(f"rstd{l}_", 4) for l in range(4)]
        nmr = {l: slots(f"nmr{l}_", 2) for l in (1, 2, 3)}
        rinv = slots("rinv", 2)
        absum = slots("absum", 2)
        mask = slots("mask", 2)

        X = [X0, X1, X2, X3]
        ring = [ctx.enter_context(nc.psum_tensor(f"ring{g}", [P, C], FP)) for g in range(SLOTS)]
        pair = [ctx.enter_context(nc.psum_tensor(f"pair{i}", [P, 2, 512], FP)) for i in range(2)]

        xT_loaded, adj_loaded = sem4("xT_loaded"), sem4("adj_loaded")
        x_loaded, adj3_loaded = sem4("x_loaded"), sem4("adj3_loaded")
        s1_done, s2_done, s3_done, s4_done = sem("s1_done"), sem("s2_done"), sem4("s3_done"), sem("s4_done")
        s5_done, s6_done, s7_done = sem4("s5_done"), sem("s6_done"), sem4("s7_done")
        s8a_done, s8b_done, s9_done = sem("s8a_done"), sem("s8b_done"), sem("s9_done")
        s10_done, s11_done = sem("s10_done"), sem("s11_done")
        adj_hi_ready, adj_ready = sem("adj_hi_ready"), sem("adj_ready")
        xb_ready = sem("xb_ready")
        h_hi_ready, h_ready = sem("h_hi_ready"), sem("h_ready")
        deg_ready, z0_ready = sem("deg_ready"), sem("z0_ready")
        y_ready = [sem4(f"y{l}_ready") for l in range(4)]
        st_ready = [sem(f"st{l}_ready") for l in range(4)]
        mv_ready = [sem(f"mv{l}_ready") for l in range(4)]
        nm_ready = [sem(f"nm{l}_ready") for l in range(4)]
        rstd_ready = [sem(f"rstd{l}_ready") for l in range(4)]
        rstdm_ready = sem("rstdm_ready")
        nmr_ready = {l: sem(f"nmr{l}_ready") for l in (1, 2, 3)}
        x_ready = [sem4(f"x{l}_ready") for l in range(4)]
        x1_hi_ready, x1_lo_ready = sem("x1_hi_ready"), sem("x1_lo_ready")
        absum_ready, mask_ready = sem4("absum_ready"), sem("mask_ready")
        t1_hi_ready, t1_ready = sem("t1_hi_ready"), sem("t1_ready")
        xd_hi_ready, xd_lo_ready = sem("xd_hi_ready"), sem("xd_lo_ready")
        dsum_ready, dhi_ready, diag_ready = sem("dsum_ready"), sem("dhi_ready"), sem4("diag_ready")
        t2_hi_ready, t2_ready = sem("t2_hi_ready"), sem("t2_ready")
        z2_ready = sem("z2_ready")
        x3T_hi_ready, x3T_ready = sem("x3T_hi_ready"), sem("x3T_ready")
        P0_ready = sem("P0_ready")
        P12_ready, Q_ready = sem("P12_ready"), sem("Q_ready")
        s_ready, e_ready, ex_ready, al_ready = sem("s_ready"), sem("e_ready"), sem("ex_ready"), sem("al_ready")
        xT_hi_ready, xT_ready = sem("xT_hi_ready"), sem("xT_ready")
        al_hi_ready, al_lo_ready, P2_ready = sem("al_hi_ready"), sem("al_lo_ready"), sem("P2_ready")
        Q_hi_ready, Q_lo_ready = sem("Q_hi_ready"), sem("Q_lo_ready")
        rinv0_ready, asum_ready, rinv3_ready = sem("rinv0_ready"), sem("asum_ready"), sem("rinv3_ready")
        z3_ready = sem("z3_ready")
        x3_free = sem4("x3_free")
        c_loaded, pool_c, bk_ready = sem("c_loaded"), sem("pool_c"), sem("bk_ready")
        b0_loaded, aw_loaded = sem("b0_loaded"), sem("aw_loaded")
        u_done, u_ready, e_const_ready = sem("u_done"), sem("u_ready"), sem("e_const_ready")
        w0_loaded, w0_hi_ready, w0_ready = sem("w0_loaded"), sem("w0_hi_ready"), sem("w0_ready")
        w_hi_ready, w_ready = sem("w_hi_ready"), sem("w_ready")

        def h_bank(g):
            return pair[g // 2][:, g % 2, :]

        def count(g, k):
            return SLOTS * k + g + 1

        def nodes(tile):
            return tile[:, 0:C].rearrange("p (t f) -> p t f", t=2)

        def diag(tile):
            return tile[:, :].rearrange("p (j c) -> p j c", c=P)[:, 0:4:3, :]

        def mixed(tile):
            return tile[:, :].rearrange("p (t f) -> p t f", t=2)

        u_stage = P1[3][:, 0:4].rearrange("p (t c) -> p t c", t=2)
        staged = [(W1, slice(0, F), nodes(P0[1])), (W2, slice(0, F), nodes(P0[2])),
                  (WA, slice(0, F), nodes(P0[3])), (WB, slice(0, F), nodes(P1[1])), (WB, slice(F, 2 * F), nodes(P1[2])),
                  (WA, slice(F, FA), u_stage)]
        W0_in = nodes(P0[0])
        bk_in = [X3[t][:, 0:F] for t in range(3)]
        attention_loads = [(P1[0], wvT), (aw_sb, aw), (bv_sb, bv)]
        c_loads = [(P0[1], w1), (P0[2], w2), (P0[3], wk[0]), (P1[1], wk[1]), (P1[2], wk[2])]
        AW_LOADED = 16 * (len(attention_loads) + 1)
        C_LOADED = 16 * (len(c_loads) + 4)

        block = ctx.enter_context(nc.Block())

        @block.sync
        def _(sp):
            def graph(dram, g, k):
                return dram[bass.ds(k * SLOTS + g, 1)].rearrange("a p c -> (a p) c")

            def load_xT(g, kn, before=True):
                if before:
                    sp.wait_ge(s1_done, count(g, kn - 1))
                sp.dma_start(xT_in[g][:, :], graph(xT, g, kn)).then_inc(xT_loaded[g], 16)

            def load_x(g, kn, before=True):
                if before:
                    sp.wait_ge(absum_ready[g], kn)
                sp.dma_start(X0[g][:, :], graph(x, g, kn)).then_inc(x_loaded[g], 16)

            def load_adj(g, kn, before=True):
                if before:
                    sp.wait_ge(diag_ready[g], kn)
                sp.dma_start(adj_in[g][:, :], graph(adjT, g, kn)).then_inc(adj_loaded[g], 16)

            def load_adj3(g, k, before=True):
                if before:
                    sp.wait_ge(al_ready, count(g, k - 1))
                sp.dma_start(adj3_in[g][:, :], graph(adjT, g, k)).then_inc(adj3_loaded[g], 16)

            def store(g, k):
                sp.wait_ge(x_ready[3][g], k + 1)
                sp.dma_start(graph(out, g, k), X3[g][:, :]).then_inc(x3_free[g], 16)

            def iteration(k, left):
                if left >= 2:
                    for g in range(SLOTS):
                        load_xT(g, k + 2)
                if left >= 2:
                    for g in range(SLOTS):
                        load_x(g, k + 2)
                if left >= 1:
                    for g in range(SLOTS):
                        load_adj3(g, k + 1)
                if left >= 2:
                    for g in range(SLOTS):
                        load_adj(g, k + 2)
                for g in range(SLOTS):
                    store(g, k)

            for load in (load_xT, load_adj):
                for g in range(SLOTS):
                    load(g, 0, before=False)
            for tile, dram in c_loads:
                sp.dma_start(tile[:, 0:C], dram).then_inc(c_loaded, 16)
            sp.dma_start(b2_bc[:, :], b2.to_broadcast([P, F])).then_inc(c_loaded, 16)
            for t in range(3):
                sp.dma_start(bk_in[t], bk[:, t * F:(t + 1) * F].to_broadcast([P, F])).then_inc(c_loaded, 16)
            for g in range(SLOTS):
                load_x(g, 0, before=False)
            for g in range(SLOTS):
                load_xT(g, 1)
            for g in range(SLOTS):
                load_adj3(g, 0, before=False)
            for load in (load_x, load_adj):
                for g in range(SLOTS):
                    load(g, 1)
            with sp.Fori(0, GROUPS - 2) as k:
                iteration(k, 2)
            iteration(GROUPS - 2, 1)
            iteration(GROUPS - 1, 0)
            for g in range(SLOTS):
                sp.wait_ge(x3_free[g], 16 * GROUPS + 16)

        @block.tensor
        def _(pe):
            mm = nc.tensor.matmul

            def product(dst, lhs, rhs):
                for i, o in enumerate(dst):
                    for t in range(2):
                        mm(o, lhs(1, t, i), rhs(0, t), start=t == 0, stop=False)
                        mm(o, lhs(0, t, i), rhs(1, t), start=False, stop=False)
                        last = mm(o, lhs(0, t, i), rhs(0, t), start=False, stop=t == 1)
                return last

            def cols(parts, g):
                return lambda s, t, i: parts[s][g][:, t * N + i * P:t * N + (i + 1) * P]

            def rows(parts, g):
                return lambda s, t: parts[s][g][:, t * N:(t + 1) * N]

            alpha = (alpha_hi, alpha_lo)
            adj, nod, fea = (adj_hi, adj_lo), (nod_hi, nod_lo), (fea_hi, fea_lo)

            def halves(g):
                return [ring[g][:, 0:N], ring[g][:, N:2 * N]]

            def s1(g, kn, first=False):
                pe.wait_ge(xT_ready, count(g, kn))
                if not first:
                    pe.wait_ge(Q_ready, count(2 + g // 2, kn - 2))
                elif kn == 1:
                    pe.wait_ge(z0_ready, count(2 + g // 2, 0))
                product([h_bank(g)[:, 0:N], h_bank(g)[:, N:2 * N]], cols((xT_hi, xT_lo), g),
                        lambda s, t: W0[s][:, t, :]).then_inc(s1_done, 1)

            def s2(g, kn):
                pe.wait_ge(h_ready, count(min(2 * g + 1, 3), kn))
                pe.wait_ge(adj_ready, count(g, kn))
                if g >= 2:
                    pe.wait_ge(z0_ready, count(g - 2, kn))
                product([pair[g % 2][:, i, 0:FA] for i in range(2)], cols(adj, g),
                        lambda s, t: mixed((h_hi, h_lo)[s][g])[:, t, :]).then_inc(s2_done, 1)

            def s3(g, kn, first=False):
                pe.wait_ge(x1_lo_ready, count(g, kn))
                if first and g == 0:
                    pe.wait_ge(e_const_ready, 2)
                if not first:
                    pe.wait_ge(s_ready, count(g, kn - 1))
                product(halves(g), cols(nod, g), rows(adj, g)).then_inc(s3_done[g], 1)

            def s4(g, kn):
                pe.wait_ge(w_ready, 1)
                pe.wait_ge(t1_ready, count(g, kn))
                product(halves(g), cols(fea, g), lambda s, t: W1[s][:, t, :]).then_inc(s4_done, 1)

            def s5(g, kn, first=False):
                pe.wait_ge(xd_lo_ready, count(g, kn))
                pe.wait_ge(diag_ready[g], kn + 1)
                if not first:
                    pe.wait_ge(z3_ready, count(g, kn - 1))
                product(halves(g), cols(nod, g), rows(adj, g)).then_inc(s5_done[g], 1)

            def s6(g, k):
                pe.wait_ge(t2_ready, count(g, k))
                product(halves(g), cols(fea, g), lambda s, t: W2[s][:, t, :]).then_inc(s6_done, 1)

            def s7(g, k):
                pe.wait_ge(x_ready[2][g], k + 1)
                for f in range(2):
                    for t in range(2):
                        last = nc.tensor.transpose(ring[g][:, f * N + t * P:f * N + (t + 1) * P],
                                                   nodes(X3[g])[:, t, f * P:(f + 1) * P], ident[:, :])
                last.then_inc(s7_done[g], 1)

            def s8a(g, k, last=False):
                pe.wait_ge(x3T_ready, count(g, k))
                if g >= 1:
                    pe.wait_ge(P0_ready, count(g - 1, k))
                elif not last:
                    pe.wait_ge(z0_ready, count(2, k + 1))
                product([pair[0][:, i, 0:FA] for i in range(2)], cols(fea, g),
                        lambda s, t: WA[s][:, t, :]).then_inc(s8a_done, 1)

            def s8b(g, k, last=False):
                if g >= 1:
                    pe.wait_ge(P2_ready, count(g - 1, k))
                elif not last:
                    pe.wait_ge(z0_ready, count(3, k + 1))
                product([pair[1][:, i, :] for i in range(2)], cols(fea, g),
                        lambda s, t: WB[s][:, t, :]).then_inc(s8b_done, 1)

            def s9(g, k):
                pe.wait_ge(P0_ready, count(g, k))
                for t in range(2):
                    last = nc.tensor.transpose(ring[g][:, t * P:(t + 1) * P],
                                               mixed(P0[g])[:, t, F + 1:FA].to_broadcast([P, P]), ident[:, :])
                last.then_inc(s9_done, 1)

            def s10(g, k):
                pe.wait_ge(al_lo_ready, count(g, k))
                pe.wait_ge(P2_ready, count(SLOTS - 1, k))
                if g == 0:
                    pe.wait_ge(P0_ready, count(SLOTS - 1, k))
                if g >= 2:
                    pe.wait_ge(Q_ready, count(g - 2, k))
                product([pair[g % 2][:, i, 0:FA] for i in range(2)], cols(alpha, g),
                        lambda s, t: mixed((h_hi, h_lo)[s][g])[:, t, :]).then_inc(s10_done, 1)

            def s11(g, k, last=False):
                pe.wait_ge(Q_lo_ready, count(g, k))
                if not last:
                    pe.wait_ge(y_ready[1][g], k + 2)
                product(halves(g), cols(alpha, g), lambda s, t: mixed((h_hi, h_lo)[s][g])[:, t, 0:F]).then_inc(s11_done, 1)

            def attention_vectors():
                pe.wait_ge(aw_loaded, AW_LOADED)
                for f in range(2):
                    for t in range(2):
                        mm(ring[0][:, 2 * f:2 * f + 2], P1[0][:, t * F + f * P:t * F + (f + 1) * P], aw_sb[:, t, :],
                           start=t == 0, stop=t == 1)
                for t in range(2):
                    last = mm(ring[0][:, 4:6], bv_sb[:, t:t + 1].to_broadcast([P, P]), aw_sb[:, t, :], start=t == 0, stop=t == 1)
                last.then_inc(u_done, 1)

            def first_iteration():
                for g in (0, 1):
                    s2(g, 0)
                attention_vectors()
                for g in (2, 3):
                    s2(g, 0)
                for g in (0, 1):
                    s1(g, 1, first=True)
                for g in (0, 1):
                    s3(g, 0, first=True)
                for g in (0, 1):
                    s4(g, 0)
                for g in (2, 3):
                    s3(g, 0, first=True)
                for g in (2, 3):
                    s4(g, 0)
                for g in (2, 3):
                    s1(g, 1, first=True)
                for g in range(SLOTS):
                    s5(g, 0, first=True)

            def iteration(k, ahead=True):
                for g in (0, 1, 2):
                    s6(g, k)
                s2(0, k + 1)
                s6(3, k)
                for g in (1, 2):
                    s2(g, k + 1)
                s7(0, k)
                s2(3, k + 1)
                s8a(0, k)
                s7(1, k)
                s8b(0, k)
                s9(0, k)
                s8a(1, k)
                s7(2, k)
                s3(0, k + 1)
                s9(1, k)
                s8b(1, k)
                s8a(2, k)
                s7(3, k)
                s4(0, k + 1)
                s9(2, k)
                s8b(2, k)
                s8a(3, k)
                for g in (1, 2):
                    s3(g, k + 1)
                s9(3, k)
                s8b(3, k)
                for g in (1, 2):
                    s4(g, k + 1)
                for g in (0, 1):
                    s10(g, k)
                s3(3, k + 1)
                s10(2, k)
                s11(0, k)
                s10(3, k)
                s4(3, k + 1)
                s11(1, k)
                if ahead:
                    for g in (0, 1):
                        s1(g, k + 2)
                for g in (2, 3):
                    s11(g, k)
                if ahead:
                    s1(2, k + 2)
                for g in range(SLOTS):
                    s5(g, k + 1)
                if ahead:
                    s1(3, k + 2)

            def last_iteration(k):
                for g in range(SLOTS):
                    s6(g, k)
                s7(0, k)
                s8a(0, k, last=True)
                s7(1, k)
                s8b(0, k, last=True)
                s9(0, k)
                s8a(1, k, last=True)
                s7(2, k)
                s8b(1, k, last=True)
                s8a(2, k, last=True)
                s7(3, k)
                s9(1, k)
                s8b(2, k, last=True)
                s9(2, k)
                s8a(3, k, last=True)
                s8b(3, k, last=True)
                s9(3, k)
                for g in (0, 1, 2):
                    s10(g, k)
                s11(0, k, last=True)
                s10(3, k)
                for g in (1, 2, 3):
                    s11(g, k, last=True)

            pe.wait_ge(w0_ready, 1)
            for g in range(SLOTS):
                s1(g, 0, first=True)
            first_iteration()
            with pe.Fori(0, GROUPS - 2) as k:
                iteration(k)
            iteration(GROUPS - 2, ahead=False)
            last_iteration(GROUPS - 1)

        @block.scalar
        def _(act):
            def copy(dst, src):
                return nc.scalar.activation(dst, src, ACT.Copy)

            def h_hi_part(g, kn):
                act.wait_ge(s1_done, count(g, kn))
                copy(mixed(h_hi[g])[:, :, 0:F], nodes(h_bank(g))).then_inc(h_hi_ready, 1)

            def z0(g, kn):
                act.wait_ge(rinv0_ready, count(g, kn))
                for t in range(2):
                    last = nc.scalar.activation(nodes(X1[g])[:, t, :], pair[g % 2][:, t, 0:F], ACT.Identity,
                                                scale=rinv[g][:, t:t + 1])
                last.then_inc(z0_ready, 1)

            def x1_hi(g, kn):
                act.wait_ge(x_ready[0][g], kn + 1)
                copy(nod_hi[g][:, :], X1[g][:, :]).then_inc(x1_hi_ready, 1)

            def x1_sum(g, kn):
                act.wait_ge(x_ready[0][g], kn + 1)
                for t in range(2):
                    last = nc.scalar.activation(X0[g][:, t * F:(t + 1) * F], nodes(X1[g])[:, t, :], ACT.Abs,
                                                accum_out=absum[g][:, t:t + 1])
                last.then_inc(absum_ready[g], 1)

            def xT_hi_part(g, kn):
                act.wait_ge(xT_loaded[g], 16 * kn + 16)
                copy(xT_hi[g][:, :], xT_in[g][:, :]).then_inc(xT_hi_ready, 1)

            def adj_hi_part(g, kn, first=False):
                act.wait_ge(adj_loaded[g], 16 * kn + 16)
                if not first:
                    act.wait_ge(s5_done[g], kn)
                copy(adj_hi[g][:, :], adj_in[g][:, :]).then_inc(adj_hi_ready, 1)

            def from_ring(g, done, k, dst, ready):
                act.wait_ge(done[g], k + 1)
                copy(dst[g][:, :], ring[g][:, :]).then_inc(ready, 1)

            def xd_hi(g, k):
                act.wait_ge(x_ready[1][g], k + 1)
                for t in range(2):
                    last = nc.scalar.activation(nod_hi[g][:, t * F:(t + 1) * F], nodes(X2[g])[:, t, :], ACT.Identity,
                                                scale=rstd[0][g][:, 2 + t:3 + t])
                last.then_inc(xd_hi_ready, 1)

            def diag_hi(g, k):
                act.wait_ge(dsum_ready, count(g, k))
                act.wait_ge(s3_done[g], k + 1)
                copy(diag(adj_hi[g]), diag(adj_in[g])).then_inc(dhi_ready, 1)

            def p12(g, k):
                act.wait_ge(s8b_done, count(g, k))
                copy(nodes(P1[g]), pair[1][:, :, 0:F])
                copy(mixed(h_hi[g])[:, :, 0:F], pair[1][:, :, F:2 * F]).then_inc(P12_ready, 1)

            def logits(g, k):
                act.wait_ge(s9_done, count(g, k))
                for t in range(2):
                    last = nc.scalar.activation(tmp[g][:, t * N:(t + 1) * N], ring[g][:, 0:N], ACT.Identity,
                                                bias=mixed(P0[g])[:, t, F:F + 1])
                last.then_inc(s_ready, 1)

            def exp(g, k):
                act.wait_ge(e_ready, count(g, k))
                nc.scalar.activation(tmp[g][:, :], tmp[g][:, :], ACT.Exp).then_inc(ex_ready, 1)

            def alpha_hi_part(g, k):
                act.wait_ge(al_ready, count(g, k))
                copy(alpha_hi[g][:, :], tmp[g][:, :]).then_inc(al_hi_ready, 1)

            def q_hi(g, k):
                act.wait_ge(Q_ready, count(g, k))
                copy(mixed(h_hi[g])[:, :, 0:F], nodes(P1[g])).then_inc(Q_hi_ready, 1)

            def norm(l, g, k):
                act.wait_ge(nmr_ready[l], count(g, k))
                if l == 2:
                    act.wait_ge(x3_free[g], 16 * k + 16)
                for t in range(2):
                    last = nc.scalar.activation(nodes(X[min(l + 1, 3)][g])[:, t, :], nodes(X[l][g])[:, t, :], ACT.Identity,
                                                scale=rstd[l][g][:, t:t + 1], bias=nmr[l][g][:, t:t + 1])
                last.then_inc(x_ready[l][g], 1)

            def weights_hi():
                act.wait_ge(c_loaded, C_LOADED)
                act.wait_ge(u_ready, 1)
                for w, columns, stage in staged:
                    last = copy(w[0][:, :, columns], stage)
                last.then_inc(w_hi_ready, 1)

            def first_iteration():
                for g in (0, 1, 2):
                    adj_hi_part(g, 0, first=True)
                for g in range(SLOTS):
                    h_hi_part(g, 0)
                adj_hi_part(3, 0, first=True)
                z0(0, 0)
                xT_hi_part(0, 1)
                z0(1, 0)
                weights_hi()
                xT_hi_part(1, 1)
                z0(2, 0)
                x1_hi(0, 0)
                z0(3, 0)
                x1_sum(0, 0)
                x1_hi(1, 0)
                diag_hi(0, 0)
                from_ring(0, s3_done, 0, fea_hi, t1_hi_ready)
                x1_sum(1, 0)
                xT_hi_part(2, 1)
                from_ring(1, s3_done, 0, fea_hi, t1_hi_ready)
                x1_hi(2, 0)
                x1_sum(2, 0)
                xT_hi_part(3, 1)
                x1_hi(3, 0)
                x1_sum(3, 0)
                diag_hi(1, 0)
                for g in (2, 3):
                    from_ring(g, s3_done, 0, fea_hi, t1_hi_ready)
                diag_hi(2, 0)
                norm(1, 0, 0)
                xd_hi(0, 0)
                norm(1, 1, 0)
                xd_hi(1, 0)
                diag_hi(3, 0)
                norm(1, 2, 0)
                xd_hi(2, 0)
                norm(1, 3, 0)
                xd_hi(3, 0)
                for g in range(SLOTS):
                    from_ring(g, s5_done, 0, fea_hi, t2_hi_ready)

            def iteration(k, ahead=True):
                h_hi_part(0, k + 1)
                adj_hi_part(0, k + 1)
                h_hi_part(1, k + 1)
                adj_hi_part(1, k + 1)
                for g in (2, 3):
                    h_hi_part(g, k + 1)
                for g in (2, 3):
                    adj_hi_part(g, k + 1)
                if ahead:
                    for g in (0, 1, 2):
                        xT_hi_part(g, k + 2)
                z0(0, k + 1)
                norm(2, 0, k)
                z0(1, k + 1)
                from_ring(0, s7_done, k, fea_hi, x3T_hi_ready)
                z0(2, k + 1)
                norm(2, 1, k)
                z0(3, k + 1)
                from_ring(1, s7_done, k, fea_hi, x3T_hi_ready)
                x1_hi(0, k + 1)
                norm(2, 2, k)
                logits(0, k)
                p12(0, k)
                from_ring(2, s7_done, k, fea_hi, x3T_hi_ready)
                x1_sum(0, k + 1)
                from_ring(0, s3_done, k + 1, fea_hi, t1_hi_ready)
                diag_hi(0, k + 1)
                norm(2, 3, k)
                p12(1, k)
                logits(1, k)
                from_ring(3, s7_done, k, fea_hi, x3T_hi_ready)
                x1_hi(1, k + 1)
                if ahead:
                    xT_hi_part(3, k + 2)
                for g in (0, 1):
                    exp(g, k)
                logits(2, k)
                x1_hi(2, k + 1)
                x1_sum(1, k + 1)
                alpha_hi_part(0, k)
                exp(2, k)
                p12(2, k)
                x1_hi(3, k + 1)
                from_ring(1, s3_done, k + 1, fea_hi, t1_hi_ready)
                alpha_hi_part(1, k)
                from_ring(2, s3_done, k + 1, fea_hi, t1_hi_ready)
                alpha_hi_part(2, k)
                logits(3, k)
                p12(3, k)
                norm(1, 0, k + 1)
                for g in (2, 3):
                    x1_sum(g, k + 1)
                diag_hi(1, k + 1)
                exp(3, k)
                xd_hi(0, k + 1)
                q_hi(0, k)
                alpha_hi_part(3, k)
                from_ring(3, s3_done, k + 1, fea_hi, t1_hi_ready)
                diag_hi(2, k + 1)
                for g in (1, 2, 3):
                    q_hi(g, k)
                diag_hi(3, k + 1)
                norm(1, 1, k + 1)
                xd_hi(1, k + 1)
                norm(1, 2, k + 1)
                xd_hi(2, k + 1)
                norm(1, 3, k + 1)
                xd_hi(3, k + 1)
                for g in (0, 1):
                    norm(3, g, k)
                for g in (0, 1, 2):
                    from_ring(g, s5_done, k + 1, fea_hi, t2_hi_ready)
                norm(3, 2, k)
                from_ring(3, s5_done, k + 1, fea_hi, t2_hi_ready)
                norm(3, 3, k)

            def last_iteration(k):
                norm(2, 0, k)
                from_ring(0, s7_done, k, fea_hi, x3T_hi_ready)
                norm(2, 1, k)
                from_ring(1, s7_done, k, fea_hi, x3T_hi_ready)
                norm(2, 2, k)
                p12(0, k)
                logits(0, k)
                from_ring(2, s7_done, k, fea_hi, x3T_hi_ready)
                norm(2, 3, k)
                p12(1, k)
                exp(0, k)
                logits(1, k)
                alpha_hi_part(0, k)
                from_ring(3, s7_done, k, fea_hi, x3T_hi_ready)
                exp(1, k)
                p12(2, k)
                logits(2, k)
                alpha_hi_part(1, k)
                exp(2, k)
                p12(3, k)
                alpha_hi_part(2, k)
                logits(3, k)
                exp(3, k)
                q_hi(0, k)
                alpha_hi_part(3, k)
                for g in (1, 2, 3):
                    q_hi(g, k)
                for g in range(SLOTS):
                    norm(3, g, k)

            act.dma_start(W0_in, w0.rearrange("p (t f) -> p t f", t=2)).then_inc(w0_loaded, 16)
            act.wait_ge(pool_c, 3)
            copy(absum[0][:, 0:1], minus_half[:, 0:1])
            for tile, dram in attention_loads:
                act.dma_start(tile[:, :], dram).then_inc(aw_loaded, 16)
            act.dma_start(ab_bc[:, :], ab.to_broadcast([P, 1])).then_inc(aw_loaded, 16)
            act.dma_start(b0_bc[:, :], b0.to_broadcast([P, F])).then_inc(b0_loaded, 16)
            act.wait_ge(w0_loaded, 16)
            copy(W0[0][:, :, :], W0_in).then_inc(w0_hi_ready, 1)
            for g in range(SLOTS):
                xT_hi_part(g, 0)
            first_iteration()
            with act.Fori(0, GROUPS - 2) as k:
                iteration(k)
            iteration(GROUPS - 2, ahead=False)
            last_iteration(GROUPS - 1)

        @block.gpsimd
        def _(pool):
            ts, tt = nc.gpsimd.tensor_scalar, nc.gpsimd.tensor_tensor

            def x_bias(g, kn):
                pool.wait_ge(x_loaded[g], 16 * kn + 16)
                tt(nodes(X0[g]), nodes(X0[g]), b0_bc[:, :].unsqueeze(1).to_broadcast([P, 2, F]), ALU.add).then_inc(xb_ready, 1)

            def adj_lo_part(g, kn):
                pool.wait_ge(adj_hi_ready, count(g, kn))
                tt(adj_lo[g][:, :], adj_in[g][:, :], adj_hi[g][:, :], ALU.subtract).then_inc(adj_ready, 1)

            def y0(g, kn):
                pool.wait_ge(xb_ready, count(g, kn))
                pool.wait_ge(z0_ready, count(g, kn))
                tt(X0[g][:, :], X0[g][:, :], X1[g][:, :], ALU.add).then_inc(y_ready[0][g], 1)

            def power(l, g, k):
                n = 4 if l == 0 else 2
                pool.wait_ge(nm_ready[l], count(g, k))
                if l == 0:
                    pool.wait_ge(deg_ready, count(g, k))
                tt(rstd[l][g][:, 0:n], powin[l][g][:, 0:n], minus_half[:, 0:n], ALU.pow).then_inc(rstd_ready[l], 1)

            def masked(g, k):
                pool.wait_ge(rstd_ready[1], count(g, k))
                pool.wait_ge(mask_ready, count(g, k))
                tt(rstd[1][g][:, 0:2], rstd[1][g][:, 0:2], mask[g][:, :], ALU.mult).then_inc(rstdm_ready, 1)

            def mean_scale(l, g, k):
                pool.wait_ge((rstdm_ready if l == 1 else rstd_ready[l]), count(g, k))
                tt(nmr[l][g][:, :], nmean[l][g][:, :], rstd[l][g][:, 0:2], ALU.mult).then_inc(nmr_ready[l], 1)

            def norm0(g, k):
                pool.wait_ge(pool_c, 3)
                pool.wait_ge(rstd_ready[0], count(g, k))
                for t in range(2):
                    last = ts(nodes(X1[g])[:, t, :], nodes(X0[g])[:, t, :], nmean[0][g][:, t:t + 1], rstd[0][g][:, t:t + 1],
                              ALU.add, ALU.mult)
                last.then_inc(x_ready[0][g], 1)

            def alpha(g, k):
                pool.wait_ge(ex_ready, count(g, k))
                pool.wait_ge(adj3_loaded[g], 16 * k + 16)
                tt(tmp[g][:, :], tmp[g][:, :], adj3_in[g][:, :], ALU.mult).then_inc(al_ready, 1)

            def xT_lo_part(g, kn):
                pool.wait_ge(xT_hi_ready, count(g, kn))
                tt(xT_lo[g][:, :], xT_in[g][:, :], xT_hi[g][:, :], ALU.subtract).then_inc(xT_ready, 1)

            def q_lo(g, k):
                pool.wait_ge(Q_hi_ready, count(g, k))
                tt(mixed(h_lo[g])[:, :, 0:F], nodes(P1[g]), mixed(h_hi[g])[:, :, 0:F], ALU.subtract).then_inc(Q_lo_ready, 1)

            def diag_sum(g, k):
                pool.wait_ge(adj_ready, count(g, k))
                ident2 = ident[:, :].unsqueeze(1).to_broadcast([P, 2, P])
                tt(diag(adj_in[g]), diag(adj_in[g]), ident2, ALU.add).then_inc(dsum_ready, 1)

            def diag_lo(g, k):
                pool.wait_ge(dhi_ready, count(g, k))
                tt(diag(adj_lo[g]), diag(adj_in[g]), diag(adj_hi[g]), ALU.subtract).then_inc(diag_ready[g], 1)

            def first_iteration():
                for g in (0, 1):
                    adj_lo_part(g, 0)
                diag_sum(0, 0)
                for g in (2, 3):
                    adj_lo_part(g, 0)
                for g in (1, 2):
                    diag_sum(g, 0)
                y0(0, 0)
                xT_lo_part(0, 1)
                for g in (1, 2):
                    y0(g, 0)
                xT_lo_part(1, 1)
                power(0, 0, 0)
                norm0(0, 0)
                diag_sum(3, 0)
                power(0, 1, 0)
                norm0(1, 0)
                y0(3, 0)
                power(0, 2, 0)
                norm0(2, 0)
                power(0, 3, 0)
                norm0(3, 0)
                for g in (2, 3):
                    xT_lo_part(g, 1)
                power(1, 0, 0)
                masked(0, 0)
                mean_scale(1, 0, 0)
                x_bias(0, 1)
                power(1, 1, 0)
                masked(1, 0)
                mean_scale(1, 1, 0)
                for g in (0, 1):
                    diag_lo(g, 0)
                power(1, 2, 0)
                masked(2, 0)
                mean_scale(1, 2, 0)
                power(1, 3, 0)
                diag_lo(2, 0)
                masked(3, 0)
                mean_scale(1, 3, 0)
                x_bias(1, 1)
                diag_lo(3, 0)
                for g in (2, 3):
                    x_bias(g, 1)

            def iteration(k, ahead=True):
                for g in (0, 1, 2):
                    adj_lo_part(g, k + 1)
                power(2, 0, k)
                mean_scale(2, 0, k)
                y0(0, k + 1)
                adj_lo_part(3, k + 1)
                power(2, 1, k)
                mean_scale(2, 1, k)
                y0(1, k + 1)
                power(0, 0, k + 1)
                norm0(0, k + 1)
                power(2, 2, k)
                mean_scale(2, 2, k)
                diag_sum(0, k + 1)
                y0(2, k + 1)
                if ahead:
                    xT_lo_part(0, k + 2)
                power(2, 3, k)
                mean_scale(2, 3, k)
                y0(3, k + 1)
                power(0, 1, k + 1)
                norm0(1, k + 1)
                power(0, 2, k + 1)
                norm0(2, k + 1)
                alpha(0, k)
                power(0, 3, k + 1)
                norm0(3, k + 1)
                for g in (1, 2):
                    alpha(g, k)
                power(1, 0, k + 1)
                for g in (1, 2):
                    diag_sum(g, k + 1)
                masked(0, k + 1)
                mean_scale(1, 0, k + 1)
                diag_sum(3, k + 1)
                if ahead:
                    for g in (1, 2):
                        xT_lo_part(g, k + 2)
                    x_bias(0, k + 2)
                alpha(3, k)
                q_lo(0, k)
                for g in (1, 2):
                    power(1, g, k + 1)
                for g in (1, 2):
                    masked(g, k + 1)
                mean_scale(1, 1, k + 1)
                q_lo(1, k)
                for g in (0, 1, 2):
                    diag_lo(g, k + 1)
                for g in (2, 3):
                    q_lo(g, k)
                mean_scale(1, 2, k + 1)
                diag_lo(3, k + 1)
                power(1, 3, k + 1)
                masked(3, k + 1)
                mean_scale(1, 3, k + 1)
                power(3, 0, k)
                mean_scale(3, 0, k)
                power(3, 1, k)
                mean_scale(3, 1, k)
                if ahead:
                    x_bias(1, k + 2)
                    xT_lo_part(3, k + 2)
                power(3, 2, k)
                mean_scale(3, 2, k)
                power(3, 3, k)
                mean_scale(3, 3, k)
                if ahead:
                    for g in (2, 3):
                        x_bias(g, k + 2)

            def last_iteration(k):
                power(2, 0, k)
                mean_scale(2, 0, k)
                power(2, 1, k)
                mean_scale(2, 1, k)
                power(2, 2, k)
                mean_scale(2, 2, k)
                power(2, 3, k)
                mean_scale(2, 3, k)
                for g in range(SLOTS):
                    alpha(g, k)
                for g in range(SLOTS):
                    q_lo(g, k)
                for g in (0, 1):
                    power(3, g, k)
                for g in (0, 1):
                    mean_scale(3, g, k)
                power(3, 2, k)
                mean_scale(3, 2, k)
                power(3, 3, k)
                mean_scale(3, 3, k)

            pool.memset(ident[:, :], 0.0).then_inc(pool_c, 1)
            pool.wait_ge(pool_c, 1)
            pool.affine_select(out=ident[:, :], in_=ident[:, :], compare_op=ALU.not_equal, fill=1.0, base=0,
                               pattern=[[-1, P]], channel_multiplier=1).then_inc(pool_c, 1)
            pool.memset(minus_half[:, :], -0.5).then_inc(pool_c, 1)
            first_iteration()
            with pool.Fori(0, GROUPS - 2) as k:
                iteration(k)
            iteration(GROUPS - 2, ahead=False)
            last_iteration(GROUPS - 1)

        @block.vector
        def _(dve):
            ts, tt, stt = nc.vector.tensor_scalar, nc.vector.tensor_tensor, nc.vector.scalar_tensor_tensor

            def from_ring(g, hi_ready, k, ready):
                dve.wait_ge(hi_ready, count(g, k))
                tt(fea_lo[g][:, :], ring[g][:, :], fea_hi[g][:, :], ALU.subtract).then_inc(ready, 1)

            def h_lo_part(g, kn):
                dve.wait_ge(h_hi_ready, count(g, kn))
                tt(mixed(h_lo[g])[:, :, 0:F], nodes(h_bank(g)), mixed(h_hi[g])[:, :, 0:F], ALU.subtract).then_inc(h_ready, 1)

            def statistics(l, g, k):
                dve.wait_ge(y_ready[l][g], k + 1)
                for t in range(2):
                    last = nc.vector.bn_stats(stats[l][g][:, 6 * t:6 * t + 6], nodes(X[l][g])[:, t, :])
                last.then_inc(st_ready[l], 1)

            def moments(l, g, k):
                dve.wait_ge(w0_ready, 1)
                dve.wait_ge(st_ready[l], count(g, k))
                for t in range(2):
                    last = nc.vector.bn_aggr(mv[l][g][:, 2 * t:2 * t + 2], stats[l][g][:, 6 * t:6 * t + 6])
                last.then_inc(mv_ready[l], 1)

            def variance_eps(l, g, k):
                dve.wait_ge(mv_ready[l], count(g, k))
                ts(powin[l][g][:, 0:2], mv[l][g][:, 1:4:2], EPS, None, ALU.add)
                ts(nmean[l][g][:, :], mv[l][g][:, 0:4:2], -1.0, None, ALU.mult).then_inc(nm_ready[l], 1)

            def sums0(g, kn):
                dve.wait_ge(s2_done, count(g, kn))
                sums = pair[g % 2][:, :, F]
                ts(powin[0][g][:, 2:4], sums, 1.0, None, ALU.add).then_inc(deg_ready, 1)
                nc.vector.reciprocal(rinv[g][:, :], sums).then_inc(rinv0_ready, 1)

            def alpha_lo_part(g, k):
                dve.wait_ge(al_hi_ready, count(g, k))
                tt(alpha_lo[g][:, :], tmp[g][:, :], alpha_hi[g][:, :], ALU.subtract).then_inc(al_lo_ready, 1)

            def p2_lo(g, k):
                dve.wait_ge(P12_ready, count(g, k))
                tt(mixed(h_lo[g])[:, :, 0:F], pair[1][:, :, F:2 * F], mixed(h_hi[g])[:, :, 0:F], ALU.subtract).then_inc(P2_ready, 1)

            def mask_of_x1(g, kn):
                dve.wait_ge(absum_ready[g], kn + 1)
                ts(mask[g][:, :], absum[g][:, :], 0.0, None, ALU.is_gt).then_inc(mask_ready, 1)

            def y1(g, k):
                dve.wait_ge(s4_done, count(g, k))
                dve.wait_ge(absum_ready[g], k + 1)
                stt(X1[g][:, :], ring[g][:, :], 0.0, X1[g][:, :], ALU.max, ALU.add).then_inc(y_ready[1][g], 1)

            def x1_lo(g, kn):
                dve.wait_ge(x1_hi_ready, count(g, kn))
                tt(nod_lo[g][:, :], X1[g][:, :], nod_hi[g][:, :], ALU.subtract).then_inc(x1_lo_ready, 1)

            def xd_lo(g, k):
                dve.wait_ge(xd_hi_ready, count(g, k))
                for t in range(2):
                    last = stt(nod_lo[g][:, t * F:(t + 1) * F], nodes(X2[g])[:, t, :], rstd[0][g][:, 2 + t:3 + t],
                               nod_hi[g][:, t * F:(t + 1) * F], ALU.mult, ALU.subtract)
                last.then_inc(xd_lo_ready, 1)

            def y2(g, k):
                dve.wait_ge(s6_done, count(g, k))
                for t in range(2):
                    last = stt(tmp[g][:, t * F:(t + 1) * F], ring[g][:, t * N:(t + 1) * N], rstd[0][g][:, 2 + t:3 + t], b2_bc[:, :],
                               ALU.mult, ALU.add)
                last.then_inc(z2_ready, 1)

            def y2b(g, k):
                dve.wait_ge(z2_ready, count(g, k))
                stt(X2[g][:, :], tmp[g][:, :], 0.0, X2[g][:, :], ALU.max, ALU.add).then_inc(y_ready[2][g], 1)

            def p0(g, k):
                dve.wait_ge(s8a_done, count(g, k))
                tt(mixed(P0[g]), pair[0][:, :, 0:FA], bk_bc[:, :].unsqueeze(1).to_broadcast([P, 2, FA]), ALU.add).then_inc(P0_ready, 1)

            def leaky(g, k):
                dve.wait_ge(s_ready, count(g, k))
                stt(tmp[g][:, :], tmp[g][:, :], 0.2, tmp[g][:, :], ALU.mult, ALU.max).then_inc(e_ready, 1)

            def alpha_sum(g, k):
                dve.wait_ge(s10_done, count(g, k))
                ts(rinv[g][:, :], pair[g % 2][:, :, F], 1e-12, None, ALU.add).then_inc(asum_ready, 1)

            def alpha_inverse(g, k):
                dve.wait_ge(asum_ready, count(g, k))
                nc.vector.reciprocal(rinv[g][:, :], rinv[g][:, :]).then_inc(rinv3_ready, 1)

            def q(g, k):
                dve.wait_ge(rinv3_ready, count(g, k))
                for t in range(2):
                    last = stt(nodes(P1[g])[:, t, :], pair[g % 2][:, t, 0:F], rinv[g][:, t:t + 1], nodes(P1[g])[:, t, :],
                               ALU.mult, ALU.add)
                last.then_inc(Q_ready, 1)

            def z3(g, k):
                dve.wait_ge(s11_done, count(g, k))
                for t in range(2):
                    last = stt(mixed(P0[g])[:, t, 0:F], ring[g][:, t * F:(t + 1) * F], rinv[g][:, t:t + 1], mixed(P0[g])[:, t, 0:F],
                               ALU.mult, ALU.add)
                last.then_inc(z3_ready, 1)

            def y3(g, k):
                dve.wait_ge(z3_ready, count(g, k))
                stt(nodes(X3[g]), mixed(P0[g])[:, :, 0:F], 0.0, nodes(X3[g]), ALU.max, ALU.add).then_inc(y_ready[3][g], 1)

            def first_x_bias(g):
                dve.wait_ge(b0_loaded, 16)
                dve.wait_ge(x_loaded[g], 16)
                tt(nodes(X0[g]), nodes(X0[g]), b0_bc[:, :].unsqueeze(1).to_broadcast([P, 2, F]), ALU.add).then_inc(xb_ready, 1)

            def attention_constants():
                dve.wait_ge(u_done, 1)
                dve.wait_ge(aw_loaded, AW_LOADED)
                nc.vector.tensor_copy(u_stage, ring[0][:, 0:4].rearrange("p (t c) -> p t c", t=2)).then_inc(u_ready, 1)
                ts(bk_bc[:, F:F + 1], ring[0][:, 4:5], ab_bc[:, 0:1], None, ALU.add).then_inc(e_const_ready, 1)
                dve.wait_ge(e_const_ready, 1)
                tt(bk_bc[:, F:F + 1], ring[0][:, 5:6], bk_bc[:, F:F + 1], ALU.add).then_inc(e_const_ready, 1)
                dve.wait_ge(e_const_ready, 2)

            def weights_lo():
                dve.wait_ge(c_loaded, C_LOADED)
                tt(bk_bc[:, 0:F], bk_in[0], bk_in[1], ALU.add).then_inc(bk_ready, 1)
                dve.wait_ge(bk_ready, 1)
                tt(bk_bc[:, 0:F], bk_bc[:, 0:F], bk_in[2], ALU.add).then_inc(bk_ready, 1)
                dve.wait_ge(w_hi_ready, 1)
                for w, columns, stage in staged:
                    last = tt(w[1][:, :, columns], stage, w[0][:, :, columns], ALU.subtract)
                last.then_inc(w_ready, 1)
                dve.wait_ge(bk_ready, 2)

            def first_iteration():
                for g in range(SLOTS):
                    h_lo_part(g, 0)
                sums0(0, 0)
                first_x_bias(0)
                sums0(1, 0)
                first_x_bias(1)
                attention_constants()
                sums0(2, 0)
                first_x_bias(2)
                statistics(0, 0, 0)
                moments(0, 0, 0)
                variance_eps(0, 0, 0)
                statistics(0, 1, 0)
                moments(0, 1, 0)
                variance_eps(0, 1, 0)
                weights_lo()
                sums0(3, 0)
                first_x_bias(3)
                x1_lo(0, 0)
                statistics(0, 2, 0)
                moments(0, 2, 0)
                mask_of_x1(0, 0)
                variance_eps(0, 2, 0)
                x1_lo(1, 0)
                statistics(0, 3, 0)
                from_ring(0, t1_hi_ready, 0, t1_ready)
                moments(0, 3, 0)
                variance_eps(0, 3, 0)
                from_ring(1, t1_hi_ready, 0, t1_ready)
                x1_lo(2, 0)
                y1(0, 0)
                mask_of_x1(1, 0)
                statistics(1, 0, 0)
                x1_lo(3, 0)
                moments(1, 0, 0)
                variance_eps(1, 0, 0)
                y1(1, 0)
                from_ring(2, t1_hi_ready, 0, t1_ready)
                statistics(1, 1, 0)
                from_ring(3, t1_hi_ready, 0, t1_ready)
                moments(1, 1, 0)
                variance_eps(1, 1, 0)
                y1(2, 0)
                statistics(1, 2, 0)
                mask_of_x1(2, 0)
                y1(3, 0)
                moments(1, 2, 0)
                mask_of_x1(3, 0)
                variance_eps(1, 2, 0)
                statistics(1, 3, 0)
                moments(1, 3, 0)
                variance_eps(1, 3, 0)
                for g in range(SLOTS):
                    xd_lo(g, 0)
                for g in range(SLOTS):
                    from_ring(g, t2_hi_ready, 0, t2_ready)

            def iteration(k, ahead=True):
                y2(0, k)
                for g in (0, 1):
                    h_lo_part(g, k + 1)
                y2b(0, k)
                h_lo_part(2, k + 1)
                statistics(2, 0, k)
                h_lo_part(3, k + 1)
                moments(2, 0, k)
                sums0(0, k + 1)
                variance_eps(2, 0, k)
                for g in (1, 2):
                    y2(g, k)
                y2b(1, k)
                sums0(1, k + 1)
                statistics(2, 1, k)
                sums0(2, k + 1)
                moments(2, 1, k)
                variance_eps(2, 1, k)
                statistics(0, 0, k + 1)
                from_ring(0, x3T_hi_ready, k, x3T_ready)
                y2b(2, k)
                moments(0, 0, k + 1)
                sums0(3, k + 1)
                variance_eps(0, 0, k + 1)
                statistics(2, 2, k)
                y2(3, k)
                moments(2, 2, k)
                variance_eps(2, 2, k)
                p0(0, k)
                from_ring(1, x3T_hi_ready, k, x3T_ready)
                statistics(0, 1, k + 1)
                y2b(3, k)
                x1_lo(0, k + 1)
                statistics(2, 3, k)
                p0(1, k)
                p2_lo(0, k)
                moments(2, 3, k)
                moments(0, 1, k + 1)
                variance_eps(2, 3, k)
                from_ring(2, x3T_hi_ready, k, x3T_ready)
                statistics(0, 2, k + 1)
                moments(0, 2, k + 1)
                variance_eps(0, 1, k + 1)
                mask_of_x1(0, k + 1)
                from_ring(0, t1_hi_ready, k + 1, t1_ready)
                statistics(0, 3, k + 1)
                variance_eps(0, 2, k + 1)
                leaky(0, k)
                p0(2, k)
                p2_lo(1, k)
                leaky(1, k)
                moments(0, 3, k + 1)
                y1(0, k + 1)
                x1_lo(1, k + 1)
                variance_eps(0, 3, k + 1)
                from_ring(3, x3T_hi_ready, k, x3T_ready)
                leaky(2, k)
                statistics(1, 0, k + 1)
                moments(1, 0, k + 1)
                x1_lo(2, k + 1)
                variance_eps(1, 0, k + 1)
                mask_of_x1(1, k + 1)
                p0(3, k)
                alpha_lo_part(0, k)
                p2_lo(2, k)
                from_ring(1, t1_hi_ready, k + 1, t1_ready)
                x1_lo(3, k + 1)
                from_ring(2, t1_hi_ready, k + 1, t1_ready)
                leaky(3, k)
                for g in (1, 2):
                    alpha_lo_part(g, k)
                p2_lo(3, k)
                y1(1, k + 1)
                statistics(1, 1, k + 1)
                y1(2, k + 1)
                moments(1, 1, k + 1)
                alpha_sum(0, k)
                variance_eps(1, 1, k + 1)
                alpha_inverse(0, k)
                q(0, k)
                statistics(1, 2, k + 1)
                xd_lo(0, k + 1)
                alpha_sum(1, k)
                mask_of_x1(2, k + 1)
                alpha_lo_part(3, k)
                alpha_inverse(1, k)
                moments(1, 2, k + 1)
                q(1, k)
                alpha_sum(2, k)
                variance_eps(1, 2, k + 1)
                from_ring(3, t1_hi_ready, k + 1, t1_ready)
                z3(0, k)
                alpha_inverse(2, k)
                mask_of_x1(3, k + 1)
                y3(0, k)
                alpha_sum(3, k)
                q(2, k)
                statistics(3, 0, k)
                alpha_inverse(3, k)
                y1(3, k + 1)
                q(3, k)
                z3(1, k)
                moments(3, 0, k)
                y3(1, k)
                statistics(1, 3, k + 1)
                statistics(3, 1, k)
                variance_eps(3, 0, k)
                moments(1, 3, k + 1)
                xd_lo(1, k + 1)
                variance_eps(1, 3, k + 1)
                moments(3, 1, k)
                for g in (2, 3):
                    z3(g, k)
                variance_eps(3, 1, k)
                y3(2, k)
                xd_lo(2, k + 1)
                statistics(3, 2, k)
                xd_lo(3, k + 1)
                moments(3, 2, k)
                y3(3, k)
                variance_eps(3, 2, k)
                statistics(3, 3, k)
                moments(3, 3, k)
                variance_eps(3, 3, k)
                for g in range(SLOTS):
                    from_ring(g, t2_hi_ready, k + 1, t2_ready)

            def last_iteration(k):
                y2(0, k)
                y2b(0, k)
                statistics(2, 0, k)
                moments(2, 0, k)
                variance_eps(2, 0, k)
                y2(1, k)
                y2b(1, k)
                statistics(2, 1, k)
                moments(2, 1, k)
                variance_eps(2, 1, k)
                y2(2, k)
                from_ring(0, x3T_hi_ready, k, x3T_ready)
                y2b(2, k)
                statistics(2, 2, k)
                moments(2, 2, k)
                variance_eps(2, 2, k)
                y2(3, k)
                p0(0, k)
                from_ring(1, x3T_hi_ready, k, x3T_ready)
                y2b(3, k)
                statistics(2, 3, k)
                p2_lo(0, k)
                moments(2, 3, k)
                variance_eps(2, 3, k)
                p0(1, k)
                leaky(0, k)
                from_ring(2, x3T_hi_ready, k, x3T_ready)
                p2_lo(1, k)
                p0(2, k)
                leaky(1, k)
                from_ring(3, x3T_hi_ready, k, x3T_ready)
                p2_lo(2, k)
                alpha_lo_part(0, k)
                leaky(2, k)
                p0(3, k)
                p2_lo(3, k)
                alpha_lo_part(1, k)
                leaky(3, k)
                alpha_sum(0, k)
                alpha_inverse(0, k)
                q(0, k)
                alpha_lo_part(2, k)
                alpha_sum(1, k)
                alpha_inverse(1, k)
                q(1, k)
                alpha_lo_part(3, k)
                alpha_sum(2, k)
                alpha_inverse(2, k)
                q(2, k)
                z3(0, k)
                y3(0, k)
                alpha_sum(3, k)
                alpha_inverse(3, k)
                statistics(3, 0, k)
                q(3, k)
                z3(1, k)
                moments(3, 0, k)
                y3(1, k)
                variance_eps(3, 0, k)
                statistics(3, 1, k)
                z3(2, k)
                moments(3, 1, k)
                y3(2, k)
                statistics(3, 2, k)
                variance_eps(3, 1, k)
                z3(3, k)
                moments(3, 2, k)
                y3(3, k)
                variance_eps(3, 2, k)
                statistics(3, 3, k)
                moments(3, 3, k)
                variance_eps(3, 3, k)

            nc.vector.memset(bk_bc[:, F + 1:FA], 0.0)
            for g in range(SLOTS):
                nc.vector.memset(mixed(h_hi[g])[:, :, F:FA].bitcast(FP), 1.0)
                nc.vector.memset(mixed(h_lo[g])[:, :, F:FA].bitcast(FP), 0.0).then_inc(x3_free[g], 16)
            dve.wait_ge(w0_hi_ready, 1)
            tt(W0[1][:, :, :], W0_in, W0[0][:, :, :], ALU.subtract).then_inc(w0_ready, 1)
            for g in range(SLOTS):
                dve.wait_ge(xT_hi_ready, g + 1)
                tt(xT_lo[g][:, :], xT_in[g][:, :], xT_hi[g][:, :], ALU.subtract).then_inc(xT_ready, 1)
            first_iteration()
            with dve.Fori(0, GROUPS - 2) as k:
                iteration(k)
            iteration(GROUPS - 2, ahead=False)
            last_iteration(GROUPS - 1)


def kernel(x, adj, L0_gnn_W, L0_gnn_b, L1_gnn_kernel, L2_gnn_kernel, L2_gnn_bias, L3_gnn_Wv, L3_gnn_bv, L3_gnn_aw,
           L3_gnn_ab, L3_gnn_Wk, L3_gnn_bk):
    import numpy as np
    import concourse.bacc as bacc
    from concourse.bass_utils import run_bass_kernel_spmd

    B, N, F = x.shape
    C = 2 * N

    def by_feature(w):
        w = np.asarray(w)
        return w.reshape(2, P, -1).transpose(1, 0, 2).reshape(P, -1)

    def nodes_last(a):
        return a.reshape(B, -1, P, 2).transpose(0, 1, 3, 2).reshape(B, -1, N)

    x, adj = np.asarray(x), np.asarray(adj)
    xT = nodes_last(x.transpose(0, 2, 1)).reshape(B, 2, P, N).transpose(0, 2, 1, 3).reshape(B, P, C)
    adjT = nodes_last(adj.transpose(0, 2, 1)).reshape(B, P, C)
    data = {
        "x": x.reshape(B, P, C), "xT": xT, "adjT": adjT,
        "w0": by_feature(L0_gnn_W), "w1": by_feature(L1_gnn_kernel), "w2": by_feature(L2_gnn_kernel),
        "wk": np.stack([by_feature(w) for w in np.asarray(L3_gnn_Wk)]),
        "wvT": by_feature(np.asarray(L3_gnn_Wv).T),
        "aw": by_feature(np.asarray(L3_gnn_aw).reshape(2, F).T), "bv": by_feature(np.asarray(L3_gnn_bv).reshape(F, 1)),
        "ab": np.asarray(L3_gnn_ab).reshape(1, 1), "b0": np.asarray(L0_gnn_b).reshape(1, F),
        "b2": np.asarray(L2_gnn_bias).reshape(1, F), "bk": np.asarray(L3_gnn_bk).reshape(1, 3 * F),
    }
    data = {name: np.ascontiguousarray(a) for name, a in data.items()}
    nc = bacc.Bacc("TRN2", target_bir_lowering=False, num_devices=1)
    drams = {name: nc.dram_tensor(f"{name}_dram", a.shape, mybir.dt.from_np(a.dtype), kind="ExternalInput").ap()
             for name, a in data.items()}
    out = nc.dram_tensor("out_dram", (B, P, C), FP, kind="ExternalOutput").ap()
    build(nc, out=out, **drams)
    result = run_bass_kernel_spmd(nc, [{f"{name}_dram": a for name, a in data.items()}], core_ids=[0])
    return result.results[0]["out_dram"].reshape(B, N, F)
```
